# Optimizing a Trainium2 kernel written in Bass

```python
import numpy as np
import jax
import jax.numpy as jnp

def _softmax(x, axis=-1):
    return jax.nn.softmax(x, axis=axis)

def _gelu(x):
    return jax.nn.gelu(x, approximate=True)

def _silu(x):
    return jax.nn.silu(x)

def _sigmoid(x):
    return jax.nn.sigmoid(x)

def _layernorm(x, axis=-1, eps=1e-05):
    m = jnp.mean(x, axis=axis, keepdims=True)
    v = jnp.var(x, axis=axis, keepdims=True)
    return (x - m) / jnp.sqrt(v + eps)

def _scatter_add(tgt, idx, src, axis=0):
    return tgt.at[idx].add(src)

def _segment_sum(src, seg, n):
    return jax.ops.segment_sum(src, seg, n)
kernel_name = 'mk_seq_postln_d1_jaxref_r4_f7f307'

def setup_inputs(seed: int=0):
    np.random.seed(seed)
    _w = jnp.asarray

    def _L0_attn_setup():
        import jax, jax.numpy as jnp
        import numpy as np
        N_HEAD = 16
        key = jax.random.key(seed)
        k1, k2, k3, k4, k5 = jax.random.split(key, 5)
        B, T, C = (8, 512, 256)
        hs = C // N_HEAD
        return {'ids': jax.random.normal(k1, (B, T, C), dtype=jnp.float32), 'qkv_w': jax.random.normal(k2, (3 * hs, C), dtype=jnp.float32) * C ** (-0.5), 'qkv_b': jax.random.normal(k3, (3 * hs,), dtype=jnp.float32) * 0.02, 'proj_w': jax.random.normal(k4, (C, C), dtype=jnp.float32) * C ** (-0.5), 'proj_b': jax.random.normal(k5, (C,), dtype=jnp.float32) * 0.02}
    _L0_attn_in = _L0_attn_setup()

    def _L0_ffn_setup():
        import jax, jax.numpy as jnp
        import numpy as np
        H_DIM, E_DIM = (256, 128)
        N_SHARED, N_ROUTED, TOP_K = (2, 16, 4)
        B, S = (4, 512)
        key = jax.random.key(seed)
        ks = jax.random.split(key, 6)
        sc = 1.0 / np.sqrt(H_DIM)
        ec = 1.0 / np.sqrt(E_DIM)
        return {'x': jax.random.normal(ks[0], (B, S, H_DIM), dtype=jnp.float32), 'shared_up': jax.random.uniform(ks[1], (N_SHARED, E_DIM, H_DIM), jnp.float32, -sc, sc), 'shared_down': jax.random.uniform(ks[2], (N_SHARED, H_DIM, E_DIM), jnp.float32, -ec, ec), 'routed_up': jax.random.uniform(ks[3], (N_ROUTED, E_DIM, H_DIM), jnp.float32, -sc, sc), 'routed_down': jax.random.uniform(ks[4], (N_ROUTED, H_DIM, E_DIM), jnp.float32, -ec, ec), 'router_w': jax.random.uniform(ks[5], (N_ROUTED, H_DIM), jnp.float32, -sc, sc)}
    _L0_ffn_in = _L0_ffn_setup()
    _d = {'L0_attn_ids': _L0_attn_in['ids'], 'L0_attn_qkv_w': _L0_attn_in['qkv_w'], 'L0_attn_qkv_b': _L0_attn_in['qkv_b'], 'L0_attn_proj_w': _L0_attn_in['proj_w'], 'L0_attn_proj_b': _L0_attn_in['proj_b'], 'L0_ffn_shared_up': _L0_ffn_in['shared_up'], 'L0_ffn_shared_down': _L0_ffn_in['shared_down'], 'L0_ffn_routed_up': _L0_ffn_in['routed_up'], 'L0_ffn_routed_down': _L0_ffn_in['routed_down'], 'L0_ffn_router_w': _L0_ffn_in['router_w']}
    _x0 = _d['L0_attn_ids']
    _d['L0_attn_ids'] = jax.random.normal(jax.random.fold_in(jax.random.key(seed), 1), (4, 2048, 256), dtype=_x0.dtype)
    del _x0
    return _d

def reference(L0_attn_ids, L0_attn_qkv_w, L0_attn_qkv_b, L0_attn_proj_w, L0_attn_proj_b, L0_ffn_shared_up, L0_ffn_shared_down, L0_ffn_routed_up, L0_ffn_routed_down, L0_ffn_router_w):

    def _L0_attn_ref(ids, qkv_w, qkv_b, proj_w, proj_b):
        import jax, jax.numpy as jnp
        import numpy as np
        N_HEAD = 16
        B, T, C = ids.shape
        hs = qkv_w.shape[0] // 3
        qkv = ids @ qkv_w.T + qkv_b
        q, k, v = jnp.split(qkv, 3, axis=-1)
        wei = jnp.einsum('btd,bsd->bts', q, k)
        tril = jnp.tril(jnp.ones((T, T), dtype=bool))
        wei = jnp.where(tril, wei, jnp.float32(0.0))
        out_h = jnp.einsum('bts,bsd->btd', wei, v)
        out = jnp.tile(out_h, (1, 1, N_HEAD))
        return out @ proj_w.T + proj_b

    def _L0_ffn_ref(x, shared_up, shared_down, routed_up, routed_down, router_w):
        import jax, jax.numpy as jnp
        import numpy as np
        H_DIM, E_DIM = (256, 128)
        N_SHARED, N_ROUTED, TOP_K = (2, 16, 4)
        B, S = (4, 512)
        b, s, h = x.shape
        xt = x.reshape(-1, h)
        up_s = jnp.einsum('th,seh->tse', xt, shared_up)
        shared = jnp.einsum('tse,she->th', jax.nn.gelu(up_s, approximate=False), shared_down)
        probs = jax.nn.softmax(xt @ router_w.T, axis=-1)
        topk_p, topk_i = jax.lax.top_k(probs, TOP_K)
        gate = jnp.zeros_like(probs).at[jnp.arange(xt.shape[0])[:, None], topk_i].add(topk_p)
        up_r = jnp.einsum('th,reh->tre', xt, routed_up)
        act = jax.nn.gelu(up_r, approximate=False) * gate[:, :, None]
        routed = jnp.einsum('tre,rhe->th', act, routed_down)
        return (shared + routed).reshape(b, s, h)
    x = L0_attn_ids
    x = _layernorm(x + _L0_attn_ref(x, L0_attn_qkv_w, L0_attn_qkv_b, L0_attn_proj_w, L0_attn_proj_b), axis=-1)
    x = _layernorm(x + _L0_ffn_ref(x, L0_ffn_shared_up, L0_ffn_shared_down, L0_ffn_routed_up, L0_ffn_routed_down, L0_ffn_router_w), axis=-1)
    return x

_drawn_inputs = setup_inputs


def setup_inputs(seed=0):
    import zlib

    import numpy as np

    out = dict(_drawn_inputs(seed))
    spreads = {}
    factors = {'L0_attn_proj_b': 200.0}
    for name, (base, spread) in spreads.items():
        noise = np.random.default_rng([zlib.crc32(name.encode()), seed]).standard_normal(out[name].shape)
        drawn = base * np.exp(spread * noise) if base else spread * noise
        out[name] = jnp.asarray(drawn.astype(out[name].dtype))
    for name, factor in factors.items():
        out[name] = (out[name] * factor).astype(out[name].dtype)
    return out
```

```python
from contextlib import ExitStack

import concourse.bass as bass
from concourse import mybir

ALU = mybir.AluOpType
ACT = mybir.ActivationFunctionType
AX = mybir.AxisListType
F32 = mybir.dt.float32
F32R = mybir.dt.float32r

P = 128
B, SEQ, C = 4, 2048, 256
HS = 16
HEADS = C // HS
NSH, NRT, TOPK = 2, 16, 4
NE = NSH + NRT
KH = C // P
T = 512
NCH = T // P
NT = B * SEQ // T
TPB = SEQ // T
LAG = 3
NUP = 3
RING = 6
GRP = 4
NG = NRT // GRP
PAD = 8 - TOPK
WCH = 3
EPS = 1e-5
EULER = 2.718281828459045


def build(nc, x, xt, qkv_wt, qkv_b, proj_wt, proj_b, up_t, down_t, router_t, out):
    ctx = ExitStack()
    with ctx:
        def sb(name, shape, dt=F32):
            return ctx.enter_context(nc.sbuf_tensor(name, shape, dt))

        def bank(name):
            return ctx.enter_context(nc.psum_tensor(name, [P, 512], F32))

        def sem(name):
            return ctx.enter_context(nc.semaphore(name))

        up_hi, up_lo = (sb(n, [P, NE, KH, P], F32R) for n in ("up_hi", "up_lo"))
        dn_hi, dn_lo = (sb(n, [P, NE, C], F32R) for n in ("dn_hi", "dn_lo"))
        gates = sb("gates", [P, NRT, T])
        stage = gates[:, :, :].rearrange("p r t -> p (r t)")
        w_heads = stage[0:HS, 4 * WCH * C:4 * WCH * C + HEADS * C].rearrange("d (n f) -> d n f", n=HEADS)
        x1t_hi, x1t_lo = (sb(n, [P, 2, KH, T], F32R) for n in ("x1t_hi", "x1t_lo"))
        h_gelu = sb("h_gelu", [P, NUP, T])
        h_gated = sb("h_gated", [P, NUP, T])
        h_hi, h_lo = (sb(n, [P, RING, T], F32R) for n in ("h_hi", "h_lo"))
        x_tok = sb("x_tok", [P, NCH, C])
        x_t = sb("x_t", [P, KH, T])
        x1_tok = sb("x1_tok", [P, 2, NCH, C])
        pre_ln = sb("pre_ln", [P, NCH, C])
        y_t = sb("y_t", [P, KH, T])
        out_tok = sb("out_tok", [P, NCH, C])
        w_qkv = sb("w_qkv", [P, KH, 3 * HS])
        b_qkv = sb("b_qkv", [P, 3 * HS])
        qkv = sb("qkv", [P, NCH, 3 * HS])
        q_t, k_t = sb("q_t", [HS, T]), sb("k_t", [HS, T])
        scores = sb("scores", [P, NCH, P])
        causal = sb("causal", [P, P])
        ident = sb("ident", [P, P])
        state = sb("state", [HS, NCH + 1, HS])
        keep = sb("keep", [HS, 2])
        o_t = sb("o_t", [HS + 1, T])
        w_proj = sb("w_proj", [HS + 1, C])
        w_rout = sb("w_rout", [P, KH, NRT])
        rt_hi, rt_lo = (sb(n, [P, KH, NRT], F32R) for n in ("rt_hi", "rt_lo"))
        euler = sb("euler", [P, NCH * NRT])
        mhalf = sb("mhalf", [P, NCH])
        shifted = sb("shifted", [P, NCH, NRT])
        expd = sb("expd", [P, NCH, NRT])
        lmax, lsum, linv = sb("lmax", [P, NCH]), sb("lsum", [P, NCH]), sb("linv", [P, NCH])
        probs = sb("probs", [P, NCH, NRT + PAD])
        top8 = sb("top8", [P, NCH, 8])
        chosen = sb("chosen", [P, NCH, 8])
        unchosen = sb("unchosen", [P, NCH, NRT + PAD])
        gate_tok = sb("gate_tok", [P, NCH, NRT])
        bearer = sb("bearer", [P, 1])
        gate_t = sb("gate_t", [NRT, T])
        gate_dram = nc.dram_tensor("gate_dram", [NRT, T], F32).ap()

        acc = [bank(f"acc{h}") for h in range(KH)]
        up_ps = [bank(f"up_ps{i}") for i in range(NUP)]
        m0, m1, m2 = (bank(f"m{i}") for i in range(3))

        xt_in, x_in, small_in = sem("xt_in"), sem("x_in"), sem("small_in")
        w_in = [sem(f"w_in{c}") for c in range(NE // WCH)]
        gate_out = sem("gate_out")
        gate_in = [sem(f"gate_in{g}") for g in range(NG)]
        stored = sem("stored")
        consts, w_hi_done, w_lo_done, wproj_done = sem("consts"), sem("w_hi_done"), sem("w_lo_done"), sem("wproj_done")
        up_done = sem("up_done")
        down_done = sem("down_done")
        acc0_done = sem("acc0_done")
        qkv_ps, qkt_ps, ds_ps, scores_ps = sem("qkv_ps"), sem("qkt_ps"), sem("ds_ps"), sem("scores_ps")
        ot_ps, proj_ps, x1t_ps, logits_ps = sem("ot_ps"), sem("proj_ps"), sem("x1t_ps"), sem("logits_ps")
        gatet_ps, back_ps = sem("gatet_ps"), sem("back_ps")
        gelu_done = sem("gelu_done")
        hi_done = sem("hi_done")
        qt_done, acc0_out, ot_done, gatet_done = sem("qt_done"), sem("acc0_out"), sem("ot_done"), sem("gatet_done")
        x1hi_done = sem("x1hi_done")
        gated = sem("gated")
        lo_done = sem("lo_done")
        qkv_done, kt_done, masked, acc1_out = sem("qkv_done"), sem("kt_done"), sem("masked"), sem("acc1_out")
        kept = sem("kept")
        state_done = sem("state_done")
        x1lo_done = sem("x1lo_done")
        lmax_done, shift_done, lsum_done, linv_done = sem("lmax_done"), sem("shift_done"), sem("lsum_done"), sem("linv_done")
        probs_done, chosen_done, gate_done = sem("probs_done"), sem("chosen_done"), sem("gate_done")
        top_done, repl_done = sem("top_done"), sem("repl_done")

        class Norm:

            def __init__(self, n):
                self.stats = sb(f"{n}_stats", [P, NCH, 6])
                self.sums = sb(f"{n}_sums", [P, NCH, 2])
                self.apart = sb(f"{n}_apart", [P, NCH])
                self.within = sb(f"{n}_within", [P, NCH])
                self.between = sb(f"{n}_between", [P, NCH])
                self.var = sb(f"{n}_var", [P, NCH])
                self.rstd = sb(f"{n}_rstd", [P, NCH])
                self.shift = sb(f"{n}_shift", [P, NCH])
                self.summed = sem(f"{n}_summed")
                self.stat_done = sem(f"{n}_stat_done")
                self.sums_done = sem(f"{n}_sums_done")
                self.apart_done = sem(f"{n}_apart_done")
                self.within_done = sem(f"{n}_within_done")
                self.between_done = sem(f"{n}_between_done")
                self.var_done = sem(f"{n}_var_done")
                self.rstd_done = sem(f"{n}_rstd_done")
                self.shift_done = sem(f"{n}_shift_done")
                self.done = sem(f"{n}_done")

        ln1, ln2 = Norm("ln1"), Norm("ln2")
        exp_done = sem("exp_done")

        x_v = x.rearrange("(n c p) f -> n p c f", p=P, c=NCH)
        out_v = out.rearrange("(n c p) f -> n p c f", p=P, c=NCH)
        tokens = [slice(c * P, (c + 1) * P) for c in range(NCH)]
        halves = tokens

        def wait(eng, s, count):
            if not isinstance(count, int) or count > 0:
                eng.wait_ge(s, count)

        def two_halves(ps):
            return ps[:, :].rearrange("p (c f) -> p c f", c=2)

        block = ctx.enter_context(nc.Block())

        @block.sync
        def _(sp):
            sp.dma_start(x_t[:, :, :], xt[0]).then_inc(xt_in, 16)
            sp.dma_start(w_qkv[:, :, :], qkv_wt).then_inc(small_in, 16)
            sp.dma_start(b_qkv[:, :], qkv_b.partition_broadcast(P)).then_inc(small_in, 16)
            sp.dma_start(w_heads, proj_wt).then_inc(small_in, 16)
            sp.dma_start(w_proj[HS:HS + 1, :], proj_b.rearrange("(a f) -> a f", a=1)).then_inc(small_in, 16)
            sp.dma_start(w_rout[:, :, :], router_t).then_inc(small_in, 16)
            sp.dma_start(x_tok[:, :, :], x_v[0]).then_inc(x_in, 16)
            n = WCH * C
            for c in range(NE // WCH):
                if c >= 2:
                    sp.wait_ge(w_lo_done, 1 + 2 * (c - 1))
                at = (c % 2) * 2 * n
                es = slice(c * WCH, (c + 1) * WCH)
                sp.dma_start(stage[:, at:at + n].rearrange("p (r k e) -> p r k e", r=WCH, k=KH),
                             up_t[:, es]).then_inc(w_in[c], 16)
                sp.dma_start(stage[:, at + n:at + 2 * n].rearrange("p (r f) -> p r f", r=WCH),
                             down_t[:, es]).then_inc(w_in[c], 16)

            def load_xt(p):
                wait(sp, qkv_ps, p)
                sp.dma_start(x_t[:, :, :], xt[p]).then_inc(xt_in, 16)

            def load_x(p):
                wait(sp, ln1.summed, 2 * p)
                sp.dma_start(x_tok[:, :, :], x_v[p]).then_inc(x_in, 16)

            def store(q):
                wait(sp, ln2.done, NCH * (q + 1))
                sp.dma_start(out_v[q], out_tok[:, :, :]).then_inc(stored, 16)

            def spread_gates(p):
                for g in range(NG):
                    wait(sp, gate_in[g], 16 * p)
                wait(sp, gatet_done, p + 1)
                sp.dma_start(gate_dram[:, :], gate_t[:, :]).then_inc(gate_out, 16)
                sp.wait_ge(gate_out, 16 * (p + 1))
                for g in range(NG):
                    wait(sp, gated, NRT * (p - 1) + GRP * (g + 1))
                    src = gate_dram[g * GRP:(g + 1) * GRP, :].rearrange("r t -> (r t)").partition_broadcast(P)
                    sp.dma_start(gates[:, g * GRP:(g + 1) * GRP, :].rearrange("p r t -> p (r t)"), src)\
                        .then_inc(gate_in[g], 16)

            load_xt(1)
            load_x(1)
            sp.wait_ge(w_lo_done, 1 + 2 * (NE // WCH))
            spread_gates(0)
            load_xt(2)
            load_x(2)
            spread_gates(1)
            with sp.Fori(2, NT - 1) as i:
                load_xt(i + 1)
                store(i - 2)
                load_x(i + 1)
                spread_gates(i)
            store(NT - 3)
            spread_gates(NT - 1)
            store(NT - 2)
            store(NT - 1)
            sp.wait_ge(stored, 16 * NT)

        @block.gpsimd
        def _(pool):
            pool.memset(ident[:, :], 0.0).then_inc(consts, 1)
            pool.memset(causal[:, :], 1.0).then_inc(consts, 1)
            pool.memset(euler[:, :], EULER).then_inc(consts, 1)
            pool.memset(mhalf[:, :], -0.5).then_inc(consts, 1)
            pool.memset(probs[:, :, :], -1.0).then_inc(consts, 1)
            pool.memset(chosen[:, :, :], -1.0).then_inc(consts, 1)
            pool.memset(o_t[:, :], 1.0).then_inc(consts, 1)
            pool.memset(keep[:, :], 0.0).then_inc(consts, 1)
            pool.memset(state[:, :, :], 0.0).then_inc(consts, 1)
            pool.wait_ge(consts, 9)
            pool.affine_select(out=ident[:, :], in_=ident[:, :], compare_op=ALU.not_equal, fill=1.0,
                               base=0, pattern=[[-1, P]], channel_multiplier=1).then_inc(consts, 1)
            pool.affine_select(out=causal[:, :], in_=causal[:, :], compare_op=ALU.is_ge, fill=0.0,
                               base=0, pattern=[[1, P]], channel_multiplier=-1).then_inc(consts, 1)

            def rstd(ln, n):
                wait(pool, ln.var_done, n + 1)
                pool.tensor_tensor(ln.rstd[:, :], ln.var[:, :], mhalf[:, :], ALU.pow).then_inc(ln.rstd_done, 1)

            def exps(p):
                wait(pool, shift_done, p + 1)
                pool.tensor_tensor(expd[:, :, :].rearrange("p c e -> p (c e)"), euler[:, :],
                                   shifted[:, :, :].rearrange("p c e -> p (c e)"), ALU.pow).then_inc(exp_done, 1)

            for p in (0, 1):
                rstd(ln1, p)
                exps(p)
            with pool.Fori(2, NT) as i:
                rstd(ln2, i - 2)
                rstd(ln1, i)
                exps(i)
            rstd(ln2, NT - 2)
            rstd(ln2, NT - 1)

        @block.scalar
        def _(act):
            def front_q(p):
                wait(act, qkt_ps, p + 1)
                act.activation(q_t[:, :], m1[0:HS, :], ACT.Copy).then_inc(qt_done, 1)

            def front_o(p):
                wait(act, ot_ps, p + 1)
                act.activation(o_t[0:HS, :], m1[0:HS, :], ACT.Copy).then_inc(ot_done, 1)

            def front_x1(p, par):
                wait(act, x1t_ps, p + 1)
                for h, ps in enumerate((m0, m2)):
                    act.activation(x1t_hi[:, par, h, :], ps[:, :], ACT.Copy).then_inc(x1hi_done, 1)

            def front_gate(p):
                wait(act, gatet_ps, p + 1)
                wait(act, gate_out, 16 * p)
                act.activation(gate_t[:, :], m1[0:NRT, :], ACT.Copy).then_inc(gatet_done, 1)

            def back_acc(q):
                wait(act, acc0_done, q + 1)
                wait(act, back_ps, q)
                act.activation(y_t[:, 0, :], acc[0][:, :], ACT.Copy).then_inc(acc0_out, 1)

            def high(t, u):
                g = NE * t + u
                if u < NSH:
                    wait(act, gelu_done, g + 1)
                    src = h_gelu
                else:
                    wait(act, gated, NRT * t + u - NSH + 1)
                    src = h_gated
                wait(act, down_done, g + 1 - RING)
                act.activation(h_hi[:, u % RING, :], src[:, u % NUP, :], ACT.Copy).then_inc(hi_done, 1)

            def gelu_free(t, u):
                if u < 0:
                    t, u = t - 1, u + NE
                if u < NSH:
                    wait(act, lo_done, NE * t + u + 1)
                else:
                    wait(act, gated, NRT * t + u - NSH + 1)

            def tile(t, par, first=False, last=False):
                for u in range(NE):
                    if u > 0:
                        high(t, u - 1)
                    elif not first:
                        high(t - 1, NE - 1)
                    wait(act, up_done, NE * t + u + 1)
                    if not (first and u < NUP):
                        gelu_free(t, u - NUP)
                    act.activation(h_gelu[:, u % NUP, :], up_ps[u % NUP][:, :], ACT.Gelu).then_inc(gelu_done, 1)
                    if u == LAG - 1 and not first:
                        back_acc(t - 1)
                    if not last:
                        if u == 1:
                            front_q(t + 1)
                        if u == 5:
                            front_o(t + 1)
                        if u == 10:
                            front_x1(t + 1, 1 - par)
                        if u == 15:
                            front_gate(t + 1)

            act.wait_ge(small_in, 80)
            act.activation(rt_hi[:, :, :], w_rout[:, :, :], ACT.Copy).then_inc(w_hi_done, 1)
            front_q(0)
            n = WCH * C

            def split(c):
                act.wait_ge(w_in[c], 32)
                at = (c % 2) * 2 * n
                es = slice(c * WCH, (c + 1) * WCH)
                act.activation(up_hi[:, es].rearrange("p r k e -> p (r k e)"), stage[:, at:at + n], ACT.Copy)\
                    .then_inc(w_hi_done, 1)
                act.activation(dn_hi[:, es].rearrange("p r f -> p (r f)"), stage[:, at + n:at + 2 * n], ACT.Copy)\
                    .then_inc(w_hi_done, 1)

            act.wait_ge(consts, 11)
            front_o(0)
            for c in range(2):
                split(c)
            front_x1(0, 0)
            for c in range(2, NE // WCH):
                split(c)
            front_gate(0)
            tile(0, 0, first=True)
            with act.Fori(1, NT - 1, 2) as i:
                tile(i, 1)
                tile(i + 1, 0)
            tile(NT - 1, 1, last=True)
            high(NT - 1, NE - 1)
            back_acc(NT - 1)

        @block.tensor
        def _(pe):
            def front_qkv(p):
                wait(pe, xt_in, 16 * (p + 1))
                for c in range(NCH):
                    for h in range(KH):
                        mm = pe.matmul(m0[:, c * 3 * HS:(c + 1) * 3 * HS], x_t[:, h, tokens[c]], w_qkv[:, h, :],
                                       start=h == 0, stop=h == KH - 1)
                mm.then_inc(qkv_ps, 1)

            def front_qkt(p):
                wait(pe, qkv_done, p + 1)
                wait(pe, gatet_done, p)
                for c in range(NCH):
                    pe.transpose(m1[0:HS, tokens[c]], qkv[:, c, 0:HS], ident[:, :])
                    mm = pe.transpose(m2[0:HS, tokens[c]], qkv[:, c, HS:2 * HS], ident[:, :])
                mm.then_inc(qkt_ps, 1)

            def front_ds(p):
                for c in range(NCH):
                    mm = pe.matmul(m0[0:HS, c * HS:(c + 1) * HS], qkv[:, c, HS:2 * HS], qkv[:, c, 2 * HS:3 * HS],
                                   start=True, stop=True)
                mm.then_inc(ds_ps, 1)

            def front_scores(p):
                wait(pe, qt_done, p + 1)
                wait(pe, kt_done, p + 1)
                for c in range(NCH):
                    mm = pe.matmul(m1[:, tokens[c]], k_t[:, tokens[c]], q_t[:, tokens[c]], start=True, stop=True)
                mm.then_inc(scores_ps, 1)

            def front_out(p):
                wait(pe, masked, p + 1)
                wait(pe, state_done, (NCH + 1) * (p + 1))
                for c in range(NCH):
                    pe.matmul(m1[0:HS, tokens[c]], qkv[:, c, 2 * HS:3 * HS], scores[:, c, :], start=True, stop=False)
                    mm = pe.matmul(m1[0:HS, tokens[c]], state[:, c, :], q_t[:, tokens[c]], start=False, stop=True)
                mm.then_inc(ot_ps, 1)

            def front_proj(p):
                wait(pe, ot_done, p + 1)
                wait(pe, ln2.summed, 2 * (p - 1))
                for c in range(NCH):
                    mm = pe.matmul(two_halves((m0, m2)[c // 2])[:, c % 2, :], o_t[:, tokens[c]], w_proj[:, :],
                                   start=True, stop=True)
                mm.then_inc(proj_ps, 1)

            def front_x1t(p, par):
                wait(pe, ln1.done, NCH * (p + 1))
                for h in range(KH):
                    for c in range(NCH):
                        mm = pe.transpose((m0, m2)[h][:, tokens[c]], x1_tok[:, par, c, halves[h]], ident[:, :])
                mm.then_inc(x1t_ps, 1)

            def front_logits(p, par):
                wait(pe, x1lo_done, KH * (p + 1))
                for c in range(NCH):
                    n = 0
                    for h in range(KH):
                        for a, b in ((x1t_hi, rt_hi), (x1t_hi, rt_lo), (x1t_lo, rt_hi)):
                            mm = pe.matmul(m1[:, c * NRT:(c + 1) * NRT], a[:, par, h, tokens[c]], b[:, h, :],
                                           start=n == 0, stop=n == 3 * KH - 1)
                            n += 1
                mm.then_inc(logits_ps, 1)

            def front_gatet(p):
                wait(pe, gate_done, p + 1)
                for c in range(NCH):
                    mm = pe.transpose(m1[0:NRT, tokens[c]], gate_tok[:, c, :], ident[:, :])
                mm.then_inc(gatet_ps, 1)

            def back(q):
                wait(pe, acc0_out, q + 1)
                wait(pe, acc1_out, q + 1)
                wait(pe, ln2.summed, 2 * q)
                for c in range(NCH):
                    for h in range(KH):
                        mm = pe.transpose(two_halves((m0, m2)[c // 2])[:, c % 2, halves[h]], y_t[:, h, tokens[c]],
                                          ident[:, :])
                mm.then_inc(back_ps, 1)

            def up(t, u, par):
                if u == 0:
                    wait(pe, x1lo_done, KH * (t + 1))
                n = 0
                for h in range(KH):
                    for a, b in ((up_hi, x1t_hi), (up_hi, x1t_lo), (up_lo, x1t_hi)):
                        mm = pe.matmul(up_ps[u % NUP][:, :], a[:, u, h, :], b[:, par, h, :],
                                       start=n == 0, stop=n == 3 * KH - 1)
                        n += 1
                mm.then_inc(up_done, 1)

            def down(t, u):
                wait(pe, lo_done, NE * t + u + 1)
                if u == 0:
                    wait(pe, acc0_out, t)
                    wait(pe, acc1_out, t)
                for h in range(KH):
                    for n, (a, b) in enumerate(((dn_hi, h_hi), (dn_hi, h_lo), (dn_lo, h_hi))):
                        mm = pe.matmul(acc[h][:, :], a[:, u, halves[h]], b[:, u % RING, :],
                                       start=u == 0 and n == 0, stop=u == NE - 1 and n == 2)
                    if u == NE - 1 and h == 0:
                        mm.then_inc(acc0_done, 1)
                mm.then_inc(down_done, 1)

            def tile(t, par, first=False, last=False):
                for u in range(NE):
                    if first and u % WCH == 0:
                        pe.wait_ge(w_lo_done, 1 + 2 * (u // WCH + 1))
                    if not (first and u < NUP):
                        wait(pe, gelu_done, NE * t + u + 1 - NUP)
                    up(t, u, par)
                    if u == 4 and not first:
                        if not last:
                            wait(pe, state_done, (NCH + 1) * (t + 2))
                        back(t - 1)
                    if not last:
                        p = t + 1
                        if u == 0:
                            front_qkv(p)
                        if u == 1:
                            front_qkt(p)
                        if u == 2:
                            front_ds(p)
                        if u == 3:
                            front_scores(p)
                        if u == 5:
                            front_out(p)
                        if u == 7:
                            front_proj(p)
                        if u == 10:
                            front_x1t(p, 1 - par)
                        if u == 12:
                            front_logits(p, 1 - par)
                        if u == 15:
                            front_gatet(p)
                    if u >= LAG:
                        down(t, u - LAG)
                    elif not first:
                        down(t - 1, NE + u - LAG)

            pe.wait_ge(small_in, 80)
            pe.wait_ge(consts, 11)
            front_qkv(0)
            front_qkt(0)
            front_ds(0)
            front_scores(0)
            front_out(0)
            pe.wait_ge(wproj_done, 1)
            front_proj(0)
            front_x1t(0, 0)
            pe.wait_ge(w_lo_done, 1)
            front_logits(0, 0)
            front_gatet(0)
            tile(0, 0, first=True)
            with pe.Fori(1, NT - 1, 2) as i:
                tile(i, 1)
                tile(i + 1, 0)
            tile(NT - 1, 1, last=True)
            for u in range(NE - LAG, NE):
                down(NT - 1, u)
            back(NT - 1)

        @block.vector
        def _(dve):
            def norm(ln, n, ps, res):
                for i in range(2):
                    dve.tensor_tensor(pre_ln[:, 2 * i:2 * i + 2, :], two_halves(ps[i]), res[:, 2 * i:2 * i + 2, :],
                                      ALU.add).then_inc(ln.summed, 1)
                for c in range(NCH):
                    if c % 2 == 0:
                        wait(dve, ln.summed, 2 * n + c // 2 + 1)
                    dve.bn_stats(ln.stats[:, c, :], pre_ln[:, c, :]).then_inc(ln.stat_done, 1)
                wait(dve, ln.stat_done, NCH * (n + 1))
                dve.tensor_tensor(ln.sums[:, :, :], ln.stats[:, :, 1:3], ln.stats[:, :, 4:6], ALU.add)\
                    .then_inc(ln.sums_done, 1)
                dve.tensor_tensor(ln.apart[:, :], ln.stats[:, :, 1], ln.stats[:, :, 4], ALU.subtract)\
                    .then_inc(ln.apart_done, 1)
                wait(dve, ln.sums_done, n + 1)
                dve.tensor_scalar(ln.within[:, :], ln.sums[:, :, 1], 1.0 / C, EPS, ALU.mult, ALU.add)\
                    .then_inc(ln.within_done, 1)
                wait(dve, ln.apart_done, n + 1)
                dve.scalar_tensor_tensor(out=ln.between[:, :], in0=ln.apart[:, :], scalar=0.25, in1=ln.apart[:, :],
                                         op0=ALU.mult, op1=ALU.mult).then_inc(ln.between_done, 1)
                wait(dve, ln.within_done, n + 1)
                wait(dve, ln.between_done, n + 1)
                dve.tensor_tensor(ln.var[:, :], ln.within[:, :], ln.between[:, :], ALU.add).then_inc(ln.var_done, 1)

            def normalise(ln, n, dst):
                wait(dve, ln.rstd_done, n + 1)
                dve.scalar_tensor_tensor(out=ln.shift[:, :], in0=ln.sums[:, :, 0], scalar=-0.5, in1=ln.rstd[:, :],
                                         op0=ALU.mult, op1=ALU.mult).then_inc(ln.shift_done, 1)
                wait(dve, ln.shift_done, n + 1)
                for c in range(NCH):
                    dve.tensor_scalar(dst[:, c, :], pre_ln[:, c, :], ln.rstd[:, c:c + 1], ln.shift[:, c:c + 1],
                                      ALU.mult, ALU.add).then_inc(ln.done, 1)

            def front_qkv(p):
                wait(dve, qkv_ps, p + 1)
                dve.tensor_tensor(qkv[:, :, :], m0[:, 0:NCH * 3 * HS].rearrange("p (c f) -> p c f", c=NCH),
                                  b_qkv[:, :].unsqueeze(1).to_broadcast([P, NCH, 3 * HS]), ALU.add)\
                    .then_inc(qkv_done, 1)

            def front_k(p):
                wait(dve, qkt_ps, p + 1)
                dve.tensor_copy(k_t[:, :], m2[0:HS, :]).then_inc(kt_done, 1)

            def front_state(p, even):
                wait(dve, ds_ps, p + 1)
                wait(dve, state_done, (NCH + 1) * p)
                wait(dve, kept, p)
                wait(dve, ot_ps, p)
                if even:
                    dve.tensor_scalar(state[:, 0, :], state[:, NCH, :], keep[:, 0:1], None, ALU.mult)\
                        .then_inc(state_done, 1)
                else:
                    dve.tensor_copy(state[:, 0, :], state[:, NCH, :]).then_inc(state_done, 1)
                for c in range(NCH):
                    wait(dve, state_done, (NCH + 1) * p + c + 1)
                    dve.tensor_tensor(state[:, c + 1, :], m0[0:HS, c * HS:(c + 1) * HS], state[:, c, :], ALU.add)\
                        .then_inc(state_done, 1)
                if even:
                    dve.tensor_scalar(keep[:, 1:2], keep[:, 0:1], -1.0, 1.0, ALU.mult, ALU.add).then_inc(kept, 1)
                else:
                    dve.tensor_copy(keep[:, 0:1], keep[:, 1:2]).then_inc(kept, 1)

            def front_mask(p):
                wait(dve, scores_ps, p + 1)
                dve.tensor_tensor(scores[:, :, :], m1[:, :].rearrange("p (c t) -> p c t", c=NCH),
                                  causal[:, :].unsqueeze(1).to_broadcast([P, NCH, P]), ALU.mult).then_inc(masked, 1)

            def front_norm(p):
                wait(dve, proj_ps, p + 1)
                wait(dve, x_in, 16 * (p + 1))
                wait(dve, ln2.done, NCH * (p - 1))
                norm(ln1, p, (m0, m2), x_tok)

            def front_x1lo(p, par):
                for h, ps in enumerate((m0, m2)):
                    wait(dve, x1hi_done, KH * p + h + 1)
                    dve.tensor_tensor(x1t_lo[:, par, h, :], ps[:, :], x1t_hi[:, par, h, :].bitcast(F32), ALU.subtract)\
                        .then_inc(x1lo_done, 1)

            def router_shift(p):
                wait(dve, logits_ps, p + 1)
                ps = m1[:, 0:NCH * NRT].rearrange("p (c e) -> p c e", c=NCH)
                dve.tensor_reduce(lmax[:, :], ps, AX.X, ALU.max).then_inc(lmax_done, 1)
                wait(dve, lmax_done, p + 1)
                dve.tensor_tensor(shifted[:, :, :], ps, lmax[:, :].unsqueeze(2).to_broadcast([P, NCH, NRT]),
                                  ALU.subtract).then_inc(shift_done, 1)

            def router_gate(p):
                wait(dve, exp_done, p + 1)
                dve.tensor_reduce(lsum[:, :], expd[:, :, :], AX.X, ALU.add).then_inc(lsum_done, 1)
                wait(dve, lsum_done, p + 1)
                dve.reciprocal(linv[:, :], lsum[:, :]).then_inc(linv_done, 1)
                wait(dve, linv_done, p + 1)
                dve.tensor_tensor(probs[:, :, 0:NRT], expd[:, :, :],
                                  linv[:, :].unsqueeze(2).to_broadcast([P, NCH, NRT]), ALU.mult).then_inc(probs_done, 1)
                wait(dve, probs_done, p + 1)
                dve.memset(bearer[:, :], 0.0)
                for c in range(NCH):
                    dve.max(top8[:, c, :], probs[:, c, 0:NRT]).then_inc(top_done, 1)
                wait(dve, top_done, NCH * (p + 1))
                dve.tensor_copy(chosen[:, :, 0:TOPK], top8[:, :, 0:TOPK]).then_inc(chosen_done, 1)
                wait(dve, chosen_done, p + 1)
                dve.memset(bearer[:, :], 0.0)
                for c in range(NCH):
                    dve.match_replace(unchosen[:, c, :], chosen[:, c, :], probs[:, c, :], 0.0).then_inc(repl_done, 1)
                wait(dve, repl_done, NCH * (p + 1))
                dve.tensor_tensor(gate_tok[:, :, :], probs[:, :, 0:NRT], unchosen[:, :, 0:NRT], ALU.subtract)\
                    .then_inc(gate_done, 1)

            def back_acc(q):
                wait(dve, down_done, NE * (q + 1))
                wait(dve, back_ps, q)
                dve.tensor_copy(y_t[:, 1, :], acc[1][:, :]).then_inc(acc1_out, 1)

            def back_norm(q, par, last=False):
                wait(dve, back_ps, q + 1)
                wait(dve, ln1.done, NCH * (q + 2) if not last else NCH * NT)
                norm(ln2, q, (m0, m2), x1_tok[:, par])

            def back_out(q):
                wait(dve, stored, 16 * q)
                normalise(ln2, q, out_tok)

            def low(t, u):
                wait(dve, hi_done, NE * t + u + 1)
                src = h_gelu if u < NSH else h_gated
                dve.tensor_tensor(h_lo[:, u % RING, :], src[:, u % NUP, :], h_hi[:, u % RING, :].bitcast(F32),
                                       ALU.subtract).then_inc(lo_done, 1)

            def tile(t, par, first=False, last=False):
                for u in range(NE):
                    if u > 0:
                        low(t, u - 1)
                    elif not first:
                        low(t - 1, NE - 1)
                    if u >= NSH:
                        r = u - NSH
                        if r % GRP == 0:
                            wait(dve, gate_in[r // GRP], 16 * (t + 1))
                        if r == 0:
                            wait(dve, lo_done, NE * t)
                        wait(dve, gelu_done, NE * t + u + 1)
                        dve.tensor_tensor(h_gated[:, u % NUP, :], h_gelu[:, u % NUP, :], gates[:, r, :], ALU.mult)\
                            .then_inc(gated, 1)
                    if not last:
                        p = t + 1
                        if u == 0:
                            front_qkv(p)
                        if u == 1:
                            front_k(p)
                        if u == 2:
                            front_state(p, even=par == 1)
                    if u == 2 and not first:
                        back_acc(t - 1)
                    if u == 4 and not first:
                        back_norm(t - 1, 1 - par, last)
                    if u == 6 and not first:
                        back_out(t - 1)
                    if not last:
                        if u == 3:
                            front_mask(p)
                        if u == 7:
                            front_norm(p)
                        if u == 8:
                            normalise(ln1, p, x1_tok[:, 1 - par])
                        if u == 10:
                            front_x1lo(p, 1 - par)
                        if u == 12:
                            router_shift(p)
                        if u == 13:
                            router_gate(p)

            n = WCH * C

            def split(c):
                at = (c % 2) * 2 * n
                es = slice(c * WCH, (c + 1) * WCH)
                for k, (hi, lo, axes) in enumerate(((up_hi, up_lo, "p r k e -> p (r k e)"),
                                                    (dn_hi, dn_lo, "p r f -> p (r f)"))):
                    dve.wait_ge(w_hi_done, 1 + 2 * c + k + 1)
                    dve.tensor_tensor(lo[:, es].rearrange(axes), stage[:, at + k * n:at + (k + 1) * n],
                                      hi[:, es].rearrange(axes).bitcast(F32), ALU.subtract).then_inc(w_lo_done, 1)

            dve.wait_ge(small_in, 80)
            dve.wait_ge(w_hi_done, 1)
            dve.tensor_tensor(rt_lo[:, :, :], w_rout[:, :, :], rt_hi[:, :, :].bitcast(F32), ALU.subtract)\
                .then_inc(w_lo_done, 1)
            dve.tensor_reduce(w_proj[0:HS, :], w_heads.rearrange("d n f -> d f n"), AX.X, ALU.add)\
                .then_inc(wproj_done, 1)
            dve.wait_ge(consts, 11)
            front_qkv(0)
            front_k(0)
            front_state(0, even=True)
            front_mask(0)
            split(0)
            front_norm(0)
            split(1)
            normalise(ln1, 0, x1_tok[:, 0])
            front_x1lo(0, 0)
            split(2)
            router_shift(0)
            split(3)
            router_gate(0)
            for c in range(4, NE // WCH):
                split(c)
            tile(0, 0, first=True)
            with dve.Fori(1, NT - 1, 2) as i:
                tile(i, 1)
                tile(i + 1, 0)
            tile(NT - 1, 1, last=True)
            low(NT - 1, NE - 1)
            back_acc(NT - 1)
            back_norm(NT - 1, 1, last=True)
            back_out(NT - 1)


def kernel(L0_attn_ids, L0_attn_qkv_w, L0_attn_qkv_b, L0_attn_proj_w, L0_attn_proj_b, L0_ffn_shared_up,
           L0_ffn_shared_down, L0_ffn_routed_up, L0_ffn_routed_down, L0_ffn_router_w):
    import numpy as np
    import concourse.bacc as bacc
    from concourse.bass_utils import run_bass_kernel_spmd

    def halved(w):
        return np.asarray(w).reshape(-1, KH, P).transpose(2, 1, 0)

    x = np.asarray(L0_attn_ids).reshape(B * SEQ, C)
    up = np.concatenate([np.asarray(L0_ffn_shared_up), np.asarray(L0_ffn_routed_up)])
    down = np.concatenate([np.asarray(L0_ffn_shared_down), np.asarray(L0_ffn_routed_down)])
    arrays = {
        "x": x,
        "xt": x.reshape(NT, T, KH, P).transpose(0, 3, 2, 1),
        "qkv_wt": halved(L0_attn_qkv_w),
        "qkv_b": np.asarray(L0_attn_qkv_b),
        "proj_wt": np.asarray(L0_attn_proj_w).reshape(C, HEADS, HS).transpose(2, 1, 0),
        "proj_b": np.asarray(L0_attn_proj_b),
        "up_t": up.reshape(NE, P, KH, P).transpose(3, 0, 2, 1),
        "down_t": down.transpose(2, 0, 1),
        "router_t": halved(L0_ffn_router_w),
    }
    arrays = {name: np.ascontiguousarray(a) for name, a in arrays.items()}
    nc = bacc.Bacc("TRN2", target_bir_lowering=False, num_devices=1)
    args = [nc.dram_tensor(name, a.shape, F32, kind="ExternalInput").ap() for name, a in arrays.items()]
    out = nc.dram_tensor("out", (B * SEQ, C), F32, kind="ExternalOutput").ap()
    build(nc, *args, out)
    got = run_bass_kernel_spmd(nc, [arrays], core_ids=[0])
    return got.results[0]["out"].reshape(B, SEQ, C)
```

```python
from contextlib import ExitStack

import concourse.bass as bass
from concourse import mybir

ALU = mybir.AluOpType
ACT = mybir.ActivationFunctionType
AX = mybir.AxisListType
F32 = mybir.dt.float32
F32R = mybir.dt.float32r

P = 128
B, SEQ, C = 4, 2048, 256
HS = 16
HEADS = C // HS
QD = 32
NQ = P // QD
NSH, NRT, TOPK = 2, 16, 4
NE = NSH + NRT
KH = C // P
T = 512
NCH = T // P
NT = B * SEQ // T
TPB = SEQ // T
LAG = 3
NUP = 3
RING = 6
GRP = 4
NG = NRT // GRP
PAD = 8 - TOPK
WCH = 3
EPS = 1e-5
EULER = 2.718281828459045


def build(nc, x, xt, qkv_wt, qkv_b, proj_wt, proj_b, up_t, down_t, router_t, out):
    ctx = ExitStack()
    with ctx:
        def sb(name, shape, dt=F32):
            return ctx.enter_context(nc.sbuf_tensor(name, shape, dt))

        def bank(name):
            return ctx.enter_context(nc.psum_tensor(name, [P, 512], F32))

        def sem(name):
            return ctx.enter_context(nc.semaphore(name))

        up_hi, up_lo = (sb(n, [P, NE, KH, P], F32R) for n in ("up_hi", "up_lo"))
        dn_hi, dn_lo = (sb(n, [P, NE, C], F32R) for n in ("dn_hi", "dn_lo"))
        gates = sb("gates", [P, NRT, T])
        stage = gates[:, :, :].rearrange("p r t -> p (r t)")
        w_heads = stage[:, 4 * WCH * C:4 * WCH * C + HEADS * C].rearrange("d (n f) -> d n f", n=HEADS)
        x1t_hi, x1t_lo = (sb(n, [P, 2, KH, T], F32R) for n in ("x1t_hi", "x1t_lo"))
        h_gelu = sb("h_gelu", [P, NUP, T])
        h_hi, h_lo = (sb(n, [P, RING, T], F32R) for n in ("h_hi", "h_lo"))
        x_tok = sb("x_tok", [P, NCH, C])
        x_t = sb("x_t", [P, KH, T])
        x1_tok = sb("x1_tok", [P, 2, NCH, C])
        pre_ln = sb("pre_ln", [P, NCH, C])
        y_t = sb("y_t", [P, KH, T])
        out_tok = sb("out_tok", [P, NCH, C])
        w_rout = out_tok[:, 0, 0:KH * NRT].rearrange("p (k e) -> p k e", k=KH)
        w_qkv = sb("w_qkv", [P, KH, 3 * HS])
        b_qkv = sb("b_qkv", [P, 3 * HS])
        qkv = sb("qkv", [P, 3, NCH, NQ, QD])
        q_t = sb("q_t", [HS + 1, T])
        q_st, k_st = sb("q_st", [P, T], F32R), sb("k_st", [P, T], F32R)
        o_st, w_st = sb("o_st", [P, T], F32R), sb("w_st", [P, C], F32R)
        w_proj = sb("w_proj", [P, C])
        scores = sb("scores", [P, NCH, P])
        causal = sb("causal", [P, P])
        ident = sb("ident", [P, P])
        state = sb("state", [HS, NCH + 1, HS])
        state_rep = sb("state_rep", [HS + 1, NCH, NQ, QD])
        keep = sb("keep", [HS, 2])
        rt_st = sb("rt_st", [P, KH, P], F32R)
        lg_t = sb("lg_t", [P, T])
        logits = sb("logits", [P, NCH, NRT])
        euler = sb("euler", [P, NCH * NRT])
        mhalf = sb("mhalf", [P, NCH])
        shifted = sb("shifted", [P, NCH, NRT])
        expd = sb("expd", [P, NCH, NRT])
        lmax, lsum, linv = sb("lmax", [P, NCH]), sb("lsum", [P, NCH]), sb("linv", [P, NCH])
        probs = sb("probs", [P, NCH, NRT + PAD])
        top8 = sb("top8", [P, NCH, 8])
        chosen = sb("chosen", [P, NCH, 8])
        unchosen = sb("unchosen", [P, NCH, NRT + PAD])
        gate_tok = sb("gate_tok", [P, NCH, NRT])
        bearer = sb("bearer", [P, 1])
        gate_t = sb("gate_t", [NRT, T])
        gate_dram = nc.dram_tensor("gate_dram", [NRT, T], F32).ap()

        acc = [bank(f"acc{h}") for h in range(KH)]
        up_ps = [bank(f"up_ps{i}") for i in range(NUP)]
        m0, m1, m2 = (bank(f"m{i}") for i in range(3))

        xt_in, x_in, small_in, heads_in = sem("xt_in"), sem("x_in"), sem("small_in"), sem("heads_in")
        w_in = [sem(f"w_in{c}") for c in range(NE // WCH)]
        gate_out = sem("gate_out")
        gate_in = [sem(f"gate_in{g}") for g in range(NG)]
        out_dma = sem("out_dma")
        CONSTS = 16
        consts, w_hi_done, w_lo_done = sem("consts"), sem("w_hi_done"), sem("w_lo_done")
        wsum_done = sem("wsum_done")
        up_done = sem("up_done")
        down_done = sem("down_done")
        acc0_done = sem("acc0_done")
        qkv_ps, qkt_ps, ds_ps, scores_ps = sem("qkv_ps"), sem("qkt_ps"), sem("ds_ps"), sem("scores_ps")
        ot_ps, proj_ps, x1t_ps = sem("ot_ps"), sem("proj_ps"), sem("x1t_ps")
        lgt_ps, logits_ps = sem("lgt_ps"), sem("logits_ps")
        gatet_ps, back_ps = sem("gatet_ps"), sem("back_ps")
        gelu_done = sem("gelu_done")
        hi_done = sem("hi_done")
        qhi_done, khi_done, ohi_done = sem("qhi_done"), sem("khi_done"), sem("ohi_done")
        acc0_out, gatet_done, lgt_done = sem("acc0_out"), sem("gatet_done"), sem("lgt_done")
        x1hi_done = sem("x1hi_done")
        gated = sem("gated")
        lo_done = sem("lo_done")
        qkv_done = sem("qkv_done")
        qk_split, o_split = sem("qk_split"), sem("o_split")
        masked, acc1_out, rep_done = sem("masked"), sem("acc1_out"), sem("rep_done")
        kept = sem("kept")
        state_done = sem("state_done")
        x1lo_done = sem("x1lo_done")
        logits_done, lmax_done, shift_done, lsum_done, linv_done = sem("logits_done"), sem("lmax_done"), sem("shift_done"), sem("lsum_done"), sem("linv_done")
        probs_done, chosen_done, gate_done = sem("probs_done"), sem("chosen_done"), sem("gate_done")
        top_done, repl_done = sem("top_done"), sem("repl_done")

        class Norm:

            def __init__(self, n):
                self.stats = sb(f"{n}_stats", [P, NCH, 6])
                self.sums = sb(f"{n}_sums", [P, NCH, 2])
                self.apart = sb(f"{n}_apart", [P, NCH])
                self.within = sb(f"{n}_within", [P, NCH])
                self.between = sb(f"{n}_between", [P, NCH])
                self.var = sb(f"{n}_var", [P, NCH])
                self.rstd = sb(f"{n}_rstd", [P, NCH])
                self.shift = sb(f"{n}_shift", [P, NCH])
                self.summed = sem(f"{n}_summed")
                self.stat_done = sem(f"{n}_stat_done")
                self.sums_done = sem(f"{n}_sums_done")
                self.apart_done = sem(f"{n}_apart_done")
                self.within_done = sem(f"{n}_within_done")
                self.between_done = sem(f"{n}_between_done")
                self.var_done = sem(f"{n}_var_done")
                self.rstd_done = sem(f"{n}_rstd_done")
                self.shift_done = sem(f"{n}_shift_done")
                self.done = sem(f"{n}_done")

        ln1, ln2 = Norm("ln1"), Norm("ln2")
        exp_done = sem("exp_done")

        x_v = x.rearrange("(n c p) f -> n p c f", p=P, c=NCH)
        out_v = out.rearrange("(n c p) f -> n p c f", p=P, c=NCH)
        tokens = [slice(c * P, (c + 1) * P) for c in range(NCH)]
        halves = tokens

        def wait(eng, s, count):
            if not isinstance(count, int) or count > 0:
                eng.wait_ge(s, count)

        def two_halves(ps):
            return ps[:, :].rearrange("p (c f) -> p c f", c=2)

        block = ctx.enter_context(nc.Block())

        @block.sync
        def _(sp):
            sp.dma_start(x_t[:, :, :], xt[0]).then_inc(xt_in, 16)
            sp.dma_start(w_qkv[:, :, :], qkv_wt).then_inc(small_in, 16)
            sp.dma_start(b_qkv[:, :], qkv_b.partition_broadcast(P)).then_inc(small_in, 16)
            sp.wait_ge(consts, 1)
            for k in range(NQ):
                sp.dma_start(w_heads[k * QD:k * QD + HS], proj_wt).then_inc(heads_in, 16)
                sp.dma_start(w_heads[k * QD + HS:k * QD + HS + 1, 0, :], proj_b.rearrange("(a f) -> a f", a=1))\
                    .then_inc(heads_in, 16)
            sp.dma_start(w_rout, router_t).then_inc(out_dma, 16)
            sp.dma_start(x_tok[:, :, :], x_v[0]).then_inc(x_in, 16)
            n = WCH * C
            for c in range(NE // WCH):
                if c >= 2:
                    sp.wait_ge(w_lo_done, 3 + 2 * (c - 1))
                at = (c % 2) * 2 * n
                es = slice(c * WCH, (c + 1) * WCH)
                sp.dma_start(stage[:, at:at + n].rearrange("p (r k e) -> p r k e", r=WCH, k=KH),
                             up_t[:, es]).then_inc(w_in[c], 16)
                sp.dma_start(stage[:, at + n:at + 2 * n].rearrange("p (r f) -> p r f", r=WCH),
                             down_t[:, es]).then_inc(w_in[c], 16)

            def load_xt(p):
                wait(sp, qkv_ps, p)
                sp.dma_start(x_t[:, :, :], xt[p]).then_inc(xt_in, 16)

            def load_x(p):
                wait(sp, ln1.summed, 2 * p)
                sp.dma_start(x_tok[:, :, :], x_v[p]).then_inc(x_in, 16)

            def store(q):
                wait(sp, ln2.done, NCH * (q + 1))
                sp.dma_start(out_v[q], out_tok[:, :, :]).then_inc(out_dma, 16)

            def spread_gates(p):
                for g in range(NG):
                    wait(sp, gate_in[g], 16 * p)
                wait(sp, gatet_done, p + 1)
                sp.dma_start(gate_dram[:, :], gate_t[:, :]).then_inc(gate_out, 16)
                sp.wait_ge(gate_out, 16 * (p + 1))
                for g in range(NG):
                    wait(sp, gated, NRT * (p - 1) + GRP * (g + 1))
                    src = gate_dram[g * GRP:(g + 1) * GRP, :].rearrange("r t -> (r t)").partition_broadcast(P)
                    sp.dma_start(gates[:, g * GRP:(g + 1) * GRP, :].rearrange("p r t -> p (r t)"), src)\
                        .then_inc(gate_in[g], 16)

            load_xt(1)
            load_x(1)
            sp.wait_ge(w_lo_done, 3 + 2 * (NE // WCH))
            spread_gates(0)
            load_xt(2)
            load_x(2)
            spread_gates(1)
            with sp.Fori(2, NT - 1) as i:
                load_xt(i + 1)
                store(i - 2)
                load_x(i + 1)
                spread_gates(i)
            store(NT - 3)
            spread_gates(NT - 1)
            store(NT - 2)
            store(NT - 1)
            sp.wait_ge(out_dma, 16 * (NT + 1))

        @block.gpsimd
        def _(pool):
            pool.memset(w_heads, 0.0).then_inc(consts, 1)
            for buf, value in ((ident[:, :], 0.0), (causal[:, :], 1.0), (euler[:, :], EULER), (mhalf[:, :], -0.5),
                               (probs[:, :, :], -1.0), (chosen[:, :, :], -1.0), (keep[:, :], 0.0),
                               (state[:, :, :], 0.0), (qkv[:, :, :, :, :], 0.0), (state_rep[:, :, :, :], 0.0)):
                pool.memset(buf, value).then_inc(consts, 1)
            pool.memset(rt_st[:, :, :].bitcast(mybir.dt.uint32), 0).then_inc(consts, 1)
            pool.wait_ge(consts, 12)
            pool.memset(qkv[:, 0, :, :, HS:HS + 1], 1.0).then_inc(consts, 1)
            pool.affine_select(out=ident[:, :], in_=ident[:, :], compare_op=ALU.not_equal, fill=1.0,
                               base=0, pattern=[[-1, P]], channel_multiplier=1).then_inc(consts, 1)
            pool.affine_select(out=causal[:, :], in_=causal[:, :], compare_op=ALU.is_ge, fill=0.0,
                               base=0, pattern=[[1, P]], channel_multiplier=-1).then_inc(consts, 1)
            ones_at = state_rep[:, :, :, :].rearrange("p c k j -> p (c k) j")
            pool.affine_select(out=ones_at, in_=ones_at, compare_op=ALU.not_equal, fill=1.0,
                               base=-HS * (2 * QD + 1), pattern=[[0, NCH * NQ], [1, QD]],
                               channel_multiplier=2 * QD).then_inc(consts, 1)

            def rstd(ln, n):
                wait(pool, ln.var_done, n + 1)
                pool.tensor_tensor(ln.rstd[:, :], ln.var[:, :], mhalf[:, :], ALU.pow).then_inc(ln.rstd_done, 1)

            def exps(p):
                wait(pool, shift_done, p + 1)
                pool.tensor_tensor(expd[:, :, :].rearrange("p c e -> p (c e)"), euler[:, :],
                                   shifted[:, :, :].rearrange("p c e -> p (c e)"), ALU.pow).then_inc(exp_done, 1)

            for p in (0, 1):
                rstd(ln1, p)
                exps(p)
            with pool.Fori(2, NT) as i:
                rstd(ln2, i - 2)
                rstd(ln1, i)
                exps(i)
            rstd(ln2, NT - 2)
            rstd(ln2, NT - 1)

        @block.scalar
        def _(act):
            def front_qk(p):
                wait(act, qkt_ps, p + 1)
                act.activation(q_st[:, :], m1[:, :], ACT.Copy).then_inc(qhi_done, 1)
                act.activation(k_st[:, :], m2[:, :], ACT.Copy).then_inc(khi_done, 1)

            def front_o(p):
                wait(act, ot_ps, p + 1)
                act.activation(o_st[:, :], m1[:, :], ACT.Copy).then_inc(ohi_done, 1)

            def front_lgt(p):
                wait(act, lgt_ps, p + 1)
                act.activation(lg_t[:, :], m1[:, :], ACT.Copy).then_inc(lgt_done, 1)

            def front_x1(p, par):
                wait(act, x1t_ps, p + 1)
                for h, ps in enumerate((m0, m2)):
                    act.activation(x1t_hi[:, par, h, :], ps[:, :], ACT.Copy).then_inc(x1hi_done, 1)

            def front_gate(p):
                wait(act, gatet_ps, p + 1)
                wait(act, gate_out, 16 * p)
                act.activation(gate_t[:, :], m1[0:NRT, :], ACT.Copy).then_inc(gatet_done, 1)

            def back_acc(q):
                wait(act, acc0_done, q + 1)
                act.activation(y_t[:, 0, :], acc[0][:, :], ACT.Copy).then_inc(acc0_out, 1)

            def high(t, u):
                g = NE * t + u
                if u < NSH:
                    wait(act, gelu_done, g + 1)
                else:
                    wait(act, gated, NRT * t + u - NSH + 1)
                wait(act, down_done, g + 1 - RING)
                act.activation(h_hi[:, u % RING, :], h_gelu[:, u % NUP, :], ACT.Copy).then_inc(hi_done, 1)

            def tile(t, par, first=False, last=False):
                for u in range(NE):
                    if u > 0:
                        high(t, u - 1)
                    elif not first:
                        high(t - 1, NE - 1)
                    wait(act, up_done, NE * t + u + 1)
                    if not (first and u < NUP):
                        wait(act, lo_done, NE * t + u + 1 - NUP)
                    act.activation(h_gelu[:, u % NUP, :], up_ps[u % NUP][:, :], ACT.Gelu).then_inc(gelu_done, 1)
                    if u == LAG - 1 and not first:
                        back_acc(t - 1)
                    if not last:
                        if u == 1:
                            front_qk(t + 1)
                        if u == 4:
                            front_o(t + 1)
                        if u == 8:
                            front_x1(t + 1, 1 - par)
                        if u == 9:
                            front_lgt(t + 1)
                        if u == 16:
                            front_gate(t + 1)

            act.wait_ge(out_dma, 16)
            act.wait_ge(consts, CONSTS)
            act.activation(rt_st[:, :, 0:NRT], w_rout, ACT.Copy).then_inc(w_hi_done, 1)
            front_qk(0)
            n = WCH * C

            def split(c):
                act.wait_ge(w_in[c], 32)
                at = (c % 2) * 2 * n
                es = slice(c * WCH, (c + 1) * WCH)
                act.activation(up_hi[:, es].rearrange("p r k e -> p (r k e)"), stage[:, at:at + n], ACT.Copy)\
                    .then_inc(w_hi_done, 1)
                act.activation(dn_hi[:, es].rearrange("p r f -> p (r f)"), stage[:, at + n:at + 2 * n], ACT.Copy)\
                    .then_inc(w_hi_done, 1)

            act.wait_ge(wsum_done, 1)
            act.activation(w_st[:, :], w_proj[:, :], ACT.Copy).then_inc(w_hi_done, 1)
            front_o(0)
            for c in range(2):
                split(c)
            front_x1(0, 0)
            front_lgt(0)
            for c in range(2, NE // WCH):
                split(c)
            front_gate(0)
            tile(0, 0, first=True)
            with act.Fori(1, NT - 1, 2) as i:
                tile(i, 1)
                tile(i + 1, 0)
            tile(NT - 1, 1, last=True)
            high(NT - 1, NE - 1)
            back_acc(NT - 1)

        @block.tensor
        def _(pe):
            def front_qkv(p):
                wait(pe, xt_in, 16 * (p + 1))
                for c in range(NCH):
                    for h in range(KH):
                        mm = pe.matmul(m0[:, c * 3 * HS:(c + 1) * 3 * HS], x_t[:, h, tokens[c]], w_qkv[:, h, :],
                                       start=h == 0, stop=h == KH - 1)
                mm.then_inc(qkv_ps, 1)

            def front_qkt(p):
                wait(pe, qkv_done, 3 * (p + 1))
                wait(pe, gatet_done, p)
                for c in range(NCH):
                    pe.transpose(m1[:, tokens[c]], qkv[:, 0, c].rearrange("p k j -> p (k j)"), ident[:, :])
                    mm = pe.transpose(m2[:, tokens[c]], qkv[:, 1, c].rearrange("p k j -> p (k j)"), ident[:, :])
                mm.then_inc(qkt_ps, 1)

            def front_ds(p):
                for c in range(NCH):
                    mm = pe.matmul(m0[0:HS, c * HS:(c + 1) * HS], qkv[:, 1, c, 0, 0:HS], qkv[:, 2, c, 0, 0:HS],
                                   start=True, stop=True)
                mm.then_inc(ds_ps, 1)

            def front_scores(p):
                wait(pe, qk_split, 4 * (p + 1))
                for c in range(NCH):
                    mm = pe.matmul(m1[:, tokens[c]], k_st[:, tokens[c]], q_st[:, tokens[c]], start=True, stop=True)
                mm.then_inc(scores_ps, 1)

            def front_out(p):
                wait(pe, masked, p + 1)
                wait(pe, rep_done, p + 1)
                for c in range(NCH):
                    pe.matmul(m1[:, tokens[c]], qkv[:, 2, c].rearrange("p k j -> p (k j)"), scores[:, c, :],
                              start=True, stop=False)
                    mm = pe.matmul(m1[:, tokens[c]], state_rep[:, c].rearrange("p k j -> p (k j)"), q_t[:, tokens[c]],
                                   start=False, stop=True)
                mm.then_inc(ot_ps, 1)

            def front_proj(p):
                wait(pe, o_split, p + 1)
                wait(pe, ln2.summed, 2 * (p - 1))
                for c in range(NCH):
                    mm = pe.matmul(two_halves((m0, m2)[c // 2])[:, c % 2, :], o_st[:, tokens[c]], w_st[:, :],
                                   start=True, stop=True)
                mm.then_inc(proj_ps, 1)

            def front_x1t(p, par):
                wait(pe, ln1.done, NCH * (p + 1))
                for h in range(KH):
                    for c in range(NCH):
                        mm = pe.transpose((m0, m2)[h][:, tokens[c]], x1_tok[:, par, c, halves[h]], ident[:, :])
                mm.then_inc(x1t_ps, 1)

            def front_lgt(p, par):
                wait(pe, x1lo_done, KH * (p + 1))
                for h in range(KH):
                    for n, b in enumerate((x1t_hi, x1t_lo)):
                        mm = pe.matmul(m1[:, :], rt_st[:, h, :], b[:, par, h, :], start=h + n == 0, stop=h + n == KH)
                mm.then_inc(lgt_ps, 1)

            def front_logits(p):
                wait(pe, lgt_done, p + 1)
                for c in range(NCH):
                    mm = pe.transpose(m1[:, tokens[c]], lg_t[:, tokens[c]], ident[:, :])
                mm.then_inc(logits_ps, 1)

            def front_gatet(p):
                wait(pe, gate_done, p + 1)
                for c in range(NCH):
                    mm = pe.transpose(m1[0:NRT, tokens[c]], gate_tok[:, c, :], ident[:, :])
                mm.then_inc(gatet_ps, 1)

            def back(q, last=False):
                wait(pe, acc0_out, q + 1)
                wait(pe, acc1_out, q + 1)
                if last:
                    pe.wait_ge(ln2.summed, 2 * q)
                for c in range(NCH):
                    for h in range(KH):
                        mm = pe.transpose(two_halves((m0, m2)[c // 2])[:, c % 2, halves[h]], y_t[:, h, tokens[c]],
                                          ident[:, :])
                mm.then_inc(back_ps, 1)

            def up(t, u, par):
                if u == 0:
                    wait(pe, x1lo_done, KH * (t + 1))
                n = 0
                for h in range(KH):
                    for a, b in ((up_hi, x1t_hi), (up_hi, x1t_lo), (up_lo, x1t_hi)):
                        mm = pe.matmul(up_ps[u % NUP][:, :], a[:, u, h, :], b[:, par, h, :],
                                       start=n == 0, stop=n == 3 * KH - 1)
                        n += 1
                mm.then_inc(up_done, 1)

            def down(t, u):
                wait(pe, lo_done, NE * t + u + 1)
                if u == 0:
                    wait(pe, acc0_out, t)
                    wait(pe, acc1_out, t)
                for h in range(KH):
                    for n, (a, b) in enumerate(((dn_hi, h_hi), (dn_hi, h_lo), (dn_lo, h_hi))):
                        mm = pe.matmul(acc[h][:, :], a[:, u, halves[h]], b[:, u % RING, :],
                                       start=u == 0 and n == 0, stop=u == NE - 1 and n == 2)
                    if u == NE - 1 and h == 0:
                        mm.then_inc(acc0_done, 1)
                mm.then_inc(down_done, 1)

            def tile(t, par, first=False, last=False):
                for u in range(NE):
                    if first and u % WCH == 0:
                        pe.wait_ge(w_lo_done, 3 + 2 * (u // WCH + 1))
                    if not (first and u < NUP):
                        wait(pe, gelu_done, NE * t + u + 1 - NUP)
                    up(t, u, par)
                    p = t + 1
                    if not last:
                        if u == 0:
                            front_qkv(p)
                        if u == 1:
                            front_qkt(p)
                        if u == 2:
                            front_ds(p)
                        if u == 3:
                            front_scores(p)
                    if u == 3 and not first:
                        if not last:
                            wait(pe, state_done, (NCH + 1) * (p + 1))
                        back(t - 1)
                    if not last:
                        if u == 4:
                            front_out(p)
                        if u == 5:
                            front_proj(p)
                        if u == 8:
                            front_x1t(p, 1 - par)
                        if u == 9:
                            front_lgt(p, 1 - par)
                        if u == 10:
                            front_logits(p)
                        if u == 16:
                            front_gatet(p)
                    if u >= LAG:
                        down(t, u - LAG)
                    elif not first:
                        down(t - 1, NE + u - LAG)

            pe.wait_ge(small_in, 32)
            pe.wait_ge(consts, CONSTS)
            front_qkv(0)
            front_qkt(0)
            front_ds(0)
            front_scores(0)
            front_out(0)
            pe.wait_ge(w_lo_done, 3)
            front_proj(0)
            front_x1t(0, 0)
            front_lgt(0, 0)
            front_logits(0)
            front_gatet(0)
            tile(0, 0, first=True)
            with pe.Fori(1, NT - 1, 2) as i:
                tile(i, 1)
                tile(i + 1, 0)
            tile(NT - 1, 1, last=True)
            for u in range(NE - LAG, NE):
                down(NT - 1, u)
            back(NT - 1, last=True)

        @block.vector
        def _(dve):
            def norm(ln, n, ps, res):
                for i in range(2):
                    dve.tensor_tensor(pre_ln[:, 2 * i:2 * i + 2, :], two_halves(ps[i]), res[:, 2 * i:2 * i + 2, :],
                                      ALU.add).then_inc(ln.summed, 1)
                for c in range(NCH):
                    if c % 2 == 0:
                        wait(dve, ln.summed, 2 * n + c // 2 + 1)
                    dve.bn_stats(ln.stats[:, c, :], pre_ln[:, c, :]).then_inc(ln.stat_done, 1)
                wait(dve, ln.stat_done, NCH * (n + 1))
                dve.tensor_tensor(ln.sums[:, :, :], ln.stats[:, :, 1:3], ln.stats[:, :, 4:6], ALU.add)\
                    .then_inc(ln.sums_done, 1)
                dve.tensor_tensor(ln.apart[:, :], ln.stats[:, :, 1], ln.stats[:, :, 4], ALU.subtract)\
                    .then_inc(ln.apart_done, 1)
                wait(dve, ln.sums_done, n + 1)
                dve.tensor_scalar(ln.within[:, :], ln.sums[:, :, 1], 1.0 / C, EPS, ALU.mult, ALU.add)\
                    .then_inc(ln.within_done, 1)
                wait(dve, ln.apart_done, n + 1)
                dve.scalar_tensor_tensor(out=ln.between[:, :], in0=ln.apart[:, :], scalar=0.25, in1=ln.apart[:, :],
                                         op0=ALU.mult, op1=ALU.mult).then_inc(ln.between_done, 1)
                wait(dve, ln.within_done, n + 1)
                wait(dve, ln.between_done, n + 1)
                dve.tensor_tensor(ln.var[:, :], ln.within[:, :], ln.between[:, :], ALU.add).then_inc(ln.var_done, 1)

            def normalise(ln, n, dst):
                wait(dve, ln.rstd_done, n + 1)
                dve.scalar_tensor_tensor(out=ln.shift[:, :], in0=ln.sums[:, :, 0], scalar=-0.5, in1=ln.rstd[:, :],
                                         op0=ALU.mult, op1=ALU.mult).then_inc(ln.shift_done, 1)
                wait(dve, ln.shift_done, n + 1)
                for c in range(NCH):
                    dve.tensor_scalar(dst[:, c, :], pre_ln[:, c, :], ln.rstd[:, c:c + 1], ln.shift[:, c:c + 1],
                                      ALU.mult, ALU.add).then_inc(ln.done, 1)

            def front_qkv(p):
                wait(dve, qkv_ps, p + 1)
                ps = m0[:, 0:NCH * 3 * HS].rearrange("p (c f) -> p c f", c=NCH)
                for i in range(3):
                    part = slice(i * HS, (i + 1) * HS)
                    dve.tensor_tensor(qkv[:, i, :, :, 0:HS],
                                      ps[:, :, part].unsqueeze(2).to_broadcast([P, NCH, NQ, HS]),
                                      b_qkv[:, part].unsqueeze(1).unsqueeze(1).to_broadcast([P, NCH, NQ, HS]),
                                      ALU.add).then_inc(qkv_done, 1)

            def front_qk(p):
                wait(dve, qhi_done, p + 1)
                dve.tensor_copy(q_t[:, :], m1[0:HS + 1, :]).then_inc(qk_split, 1)
                lo_part(q_st, m1, 2 * QD, P).then_inc(qk_split, 1)
                wait(dve, khi_done, p + 1)
                lo_part(k_st, m2, QD, 2 * QD).then_inc(qk_split, 1)
                lo_part(k_st, m2, 3 * QD, P).then_inc(qk_split, 1)

            def lo_part(st, src, a, b):
                return dve.tensor_tensor(st[a:b, :], src[a:b, :], st[a:b, :].bitcast(F32), ALU.subtract)

            def front_o(p):
                wait(dve, ohi_done, p + 1)
                lo_part(o_st, m1, 2 * QD, P).then_inc(o_split, 1)

            def front_state(p, even):
                wait(dve, ds_ps, p + 1)
                wait(dve, state_done, (NCH + 1) * p)
                wait(dve, kept, p)
                wait(dve, ot_ps, p)
                if even:
                    dve.tensor_scalar(state[:, 0, :], state[:, NCH, :], keep[:, 0:1], None, ALU.mult)\
                        .then_inc(state_done, 1)
                else:
                    dve.tensor_copy(state[:, 0, :], state[:, NCH, :]).then_inc(state_done, 1)
                for c in range(NCH):
                    wait(dve, state_done, (NCH + 1) * p + c + 1)
                    dve.tensor_tensor(state[:, c + 1, :], m0[0:HS, c * HS:(c + 1) * HS], state[:, c, :], ALU.add)\
                        .then_inc(state_done, 1)
                wait(dve, state_done, (NCH + 1) * (p + 1))
                dve.tensor_copy(state_rep[0:HS, :, :, 0:HS],
                                state[:, 0:NCH, :].unsqueeze(2).to_broadcast([HS, NCH, NQ, HS])).then_inc(rep_done, 1)
                if even:
                    dve.tensor_scalar(keep[:, 1:2], keep[:, 0:1], -1.0, 1.0, ALU.mult, ALU.add).then_inc(kept, 1)
                else:
                    dve.tensor_copy(keep[:, 0:1], keep[:, 1:2]).then_inc(kept, 1)

            def front_mask(p):
                wait(dve, scores_ps, p + 1)
                dve.tensor_tensor(scores[:, :, :], m1[:, :].rearrange("p (c t) -> p c t", c=NCH),
                                  causal[:, :].unsqueeze(1).to_broadcast([P, NCH, P]), ALU.mult).then_inc(masked, 1)

            def front_norm(p):
                wait(dve, proj_ps, p + 1)
                wait(dve, x_in, 16 * (p + 1))
                wait(dve, ln2.done, NCH * (p - 1))
                norm(ln1, p, (m0, m2), x_tok)

            def front_x1lo(p, par):
                for h, ps in enumerate((m0, m2)):
                    wait(dve, x1hi_done, KH * p + h + 1)
                    dve.tensor_tensor(x1t_lo[:, par, h, :], ps[:, :], x1t_hi[:, par, h, :].bitcast(F32), ALU.subtract)\
                        .then_inc(x1lo_done, 1)

            def router_shift(p):
                wait(dve, logits_ps, p + 1)
                ps = m1[:, :].rearrange("p (c k j) -> p c j k", c=NCH, k=NQ)
                dve.tensor_reduce(logits[:, :, :], ps[:, :, 0:NRT, 0:2], AX.X, ALU.add).then_inc(logits_done, 1)
                wait(dve, logits_done, p + 1)
                dve.tensor_reduce(lmax[:, :], logits[:, :, :], AX.X, ALU.max).then_inc(lmax_done, 1)
                wait(dve, lmax_done, p + 1)
                dve.tensor_tensor(shifted[:, :, :], logits[:, :, :],
                                  lmax[:, :].unsqueeze(2).to_broadcast([P, NCH, NRT]), ALU.subtract)\
                    .then_inc(shift_done, 1)

            def router_gate(p):
                wait(dve, exp_done, p + 1)
                dve.tensor_reduce(lsum[:, :], expd[:, :, :], AX.X, ALU.add).then_inc(lsum_done, 1)
                wait(dve, lsum_done, p + 1)
                dve.reciprocal(linv[:, :], lsum[:, :]).then_inc(linv_done, 1)
                wait(dve, linv_done, p + 1)
                dve.tensor_tensor(probs[:, :, 0:NRT], expd[:, :, :],
                                  linv[:, :].unsqueeze(2).to_broadcast([P, NCH, NRT]), ALU.mult).then_inc(probs_done, 1)
                wait(dve, probs_done, p + 1)
                dve.memset(bearer[:, :], 0.0)
                for c in range(NCH):
                    dve.max(top8[:, c, :], probs[:, c, 0:NRT]).then_inc(top_done, 1)
                wait(dve, top_done, NCH * (p + 1))
                dve.tensor_copy(chosen[:, :, 0:TOPK], top8[:, :, 0:TOPK]).then_inc(chosen_done, 1)
                wait(dve, chosen_done, p + 1)
                dve.memset(bearer[:, :], 0.0)
                for c in range(NCH):
                    dve.match_replace(unchosen[:, c, :], chosen[:, c, :], probs[:, c, :], 0.0).then_inc(repl_done, 1)
                wait(dve, repl_done, NCH * (p + 1))
                dve.tensor_tensor(gate_tok[:, :, :], probs[:, :, 0:NRT], unchosen[:, :, 0:NRT], ALU.subtract)\
                    .then_inc(gate_done, 1)

            def back_acc(q):
                wait(dve, down_done, NE * (q + 1))
                dve.tensor_copy(y_t[:, 1, :], acc[1][:, :]).then_inc(acc1_out, 1)

            def back_norm(q, par, last=False):
                wait(dve, back_ps, q + 1)
                wait(dve, ln1.done, NCH * (q + 2) if not last else NCH * NT)
                norm(ln2, q, (m0, m2), x1_tok[:, par])

            def back_out(q):
                wait(dve, out_dma, 16 * (q + 1))
                normalise(ln2, q, out_tok)

            def low(t, u):
                wait(dve, hi_done, NE * t + u + 1)
                dve.tensor_tensor(h_lo[:, u % RING, :], h_gelu[:, u % NUP, :], h_hi[:, u % RING, :].bitcast(F32),
                                       ALU.subtract).then_inc(lo_done, 1)

            def tile(t, par, first=False, last=False):
                for u in range(NE):
                    if u > 0:
                        low(t, u - 1)
                    elif not first:
                        low(t - 1, NE - 1)
                    if u >= NSH:
                        r = u - NSH
                        if r % GRP == 0:
                            wait(dve, gate_in[r // GRP], 16 * (t + 1))
                        wait(dve, gelu_done, NE * t + u + 1)
                        dve.tensor_tensor(h_gelu[:, u % NUP, :], h_gelu[:, u % NUP, :], gates[:, r, :], ALU.mult)\
                            .then_inc(gated, 1)
                    p = t + 1
                    if not last:
                        if u == 0:
                            front_qkv(p)
                        if u == 1:
                            front_qk(p)
                        if u == 2:
                            front_state(p, even=par == 1)
                        if u == 3:
                            front_mask(p)
                    if not first:
                        if u == 2:
                            back_acc(t - 1)
                        if u == 3:
                            back_norm(t - 1, 1 - par, last)
                        if u == 4:
                            if not last:
                                front_o(p)
                            back_out(t - 1)
                    elif u == 4:
                        front_o(p)
                    if not last:
                        if u == 5:
                            front_norm(p)
                        if u == 6:
                            normalise(ln1, p, x1_tok[:, 1 - par])
                        if u == 8:
                            front_x1lo(p, 1 - par)
                        if u == 10:
                            router_shift(p)
                        if u == 15:
                            router_gate(p)

            n = WCH * C

            def split(c):
                at = (c % 2) * 2 * n
                es = slice(c * WCH, (c + 1) * WCH)
                for k, (hi, lo, axes) in enumerate(((up_hi, up_lo, "p r k e -> p (r k e)"),
                                                    (dn_hi, dn_lo, "p r f -> p (r f)"))):
                    dve.wait_ge(w_hi_done, 2 + 2 * c + k + 1)
                    dve.tensor_tensor(lo[:, es].rearrange(axes), stage[:, at + k * n:at + (k + 1) * n],
                                      hi[:, es].rearrange(axes).bitcast(F32), ALU.subtract).then_inc(w_lo_done, 1)

            dve.wait_ge(small_in, 32)
            dve.wait_ge(consts, CONSTS)
            front_qkv(0)
            dve.wait_ge(w_hi_done, 1)
            dve.tensor_tensor(rt_st[:, :, QD:QD + NRT], w_rout, rt_st[:, :, 0:NRT].bitcast(F32), ALU.subtract)\
                .then_inc(w_lo_done, 1)
            front_qk(0)
            front_state(0, even=True)
            front_mask(0)
            dve.wait_ge(heads_in, 2 * 16 * NQ)
            dve.tensor_reduce(w_proj[:, :], w_heads.rearrange("d n f -> d f n"), AX.X, ALU.add).then_inc(wsum_done, 1)
            dve.wait_ge(w_hi_done, 2)
            lo_part(w_st, w_proj, QD, 2 * QD).then_inc(w_lo_done, 1)
            lo_part(w_st, w_proj, 3 * QD, P).then_inc(w_lo_done, 1)
            front_o(0)
            split(0)
            front_norm(0)
            split(1)
            normalise(ln1, 0, x1_tok[:, 0])
            front_x1lo(0, 0)
            split(2)
            router_shift(0)
            split(3)
            router_gate(0)
            for c in range(4, NE // WCH):
                split(c)
            tile(0, 0, first=True)
            with dve.Fori(1, NT - 1, 2) as i:
                tile(i, 1)
                tile(i + 1, 0)
            tile(NT - 1, 1, last=True)
            low(NT - 1, NE - 1)
            back_acc(NT - 1)
            back_norm(NT - 1, 1, last=True)
            back_out(NT - 1)


def kernel(L0_attn_ids, L0_attn_qkv_w, L0_attn_qkv_b, L0_attn_proj_w, L0_attn_proj_b, L0_ffn_shared_up,
           L0_ffn_shared_down, L0_ffn_routed_up, L0_ffn_routed_down, L0_ffn_router_w):
    import numpy as np
    import concourse.bacc as bacc
    from concourse.bass_utils import run_bass_kernel_spmd

    def halved(w):
        return np.asarray(w).reshape(-1, KH, P).transpose(2, 1, 0)

    x = np.asarray(L0_attn_ids).reshape(B * SEQ, C)
    up = np.concatenate([np.asarray(L0_ffn_shared_up), np.asarray(L0_ffn_routed_up)])
    down = np.concatenate([np.asarray(L0_ffn_shared_down), np.asarray(L0_ffn_routed_down)])
    arrays = {
        "x": x,
        "xt": x.reshape(NT, T, KH, P).transpose(0, 3, 2, 1),
        "qkv_wt": halved(L0_attn_qkv_w),
        "qkv_b": np.asarray(L0_attn_qkv_b),
        "proj_wt": np.asarray(L0_attn_proj_w).reshape(C, HEADS, HS).transpose(2, 1, 0),
        "proj_b": np.asarray(L0_attn_proj_b),
        "up_t": up.reshape(NE, P, KH, P).transpose(3, 0, 2, 1),
        "down_t": down.transpose(2, 0, 1),
        "router_t": halved(L0_ffn_router_w),
    }
    arrays = {name: np.ascontiguousarray(a) for name, a in arrays.items()}
    nc = bacc.Bacc("TRN2", target_bir_lowering=False, num_devices=1)
    args = [nc.dram_tensor(name, a.shape, F32, kind="ExternalInput").ap() for name, a in arrays.items()]
    out = nc.dram_tensor("out", (B * SEQ, C), F32, kind="ExternalOutput").ap()
    build(nc, *args, out)
    got = run_bass_kernel_spmd(nc, [arrays], core_ids=[0])
    return got.results[0]["out"].reshape(B, SEQ, C)
```

```python
from contextlib import ExitStack

import concourse.bass as bass
from concourse import mybir

ALU = mybir.AluOpType
ACT = mybir.ActivationFunctionType
AX = mybir.AxisListType
F32 = mybir.dt.float32
F32R = mybir.dt.float32r

P = 128
B, SEQ, C = 4, 2048, 256
HS = 16
HEADS = C // HS
LEVELS = 4
assert HEADS == 1 << LEVELS
QD = 32
NQ = P // QD
NSH, NRT, TOPK = 2, 16, 4
NE = NSH + NRT
KH = C // P
T = 512
NCH = T // P
NT = B * SEQ // T
assert SEQ == 4 * T
LAG = 3
NUP = 3
RING = 6
GRP = 4
NG = NRT // GRP
PAD = 8 - TOPK
WCH = 3
NWC = NE // WCH
CHUNK = 2 * WCH * C
NSTAGE = 5
OPEN = 2 * LAG
EPS = 1e-5


def build(nc, x, xt, qkv_wt, qkv_b, proj_wt, proj_b, up_t, down_t, router_t, out):
    ctx = ExitStack()
    with ctx:
        def sb(name, shape, dt=F32):
            return ctx.enter_context(nc.sbuf_tensor(name, shape, dt))

        def bank(name):
            return ctx.enter_context(nc.psum_tensor(name, [P, 512], F32))

        def sem(name):
            return ctx.enter_context(nc.semaphore(name))

        up_hi, up_lo = (sb(n, [P, NE, KH, P], F32R) for n in ("up_hi", "up_lo"))
        dn_hi, dn_lo = (sb(n, [P, NE, C], F32R) for n in ("dn_hi", "dn_lo"))
        gates = sb("gates", [P, NRT, T])
        stage = gates[:, :, :].rearrange("p r t -> p (r t)")
        w_heads = stage[:, 2 * CHUNK:2 * CHUNK + HEADS * C].rearrange("d (n f) -> d n f", n=HEADS)
        x1t_hi, x1t_lo = (sb(n, [P, 2, KH, T], F32R) for n in ("x1t_hi", "x1t_lo"))
        h_gelu = sb("h_gelu", [P, NUP, T])
        h_hi, h_lo = (sb(n, [P, RING, T], F32R) for n in ("h_hi", "h_lo"))
        x_tok = sb("x_tok", [P, NCH, C])
        x_t = sb("x_t", [P, 2, KH, T])
        x1_tok = sb("x1_tok", [P, 2, NCH, C])
        pre_ln = sb("pre_ln", [P, NCH, C])
        out_tok = sb("out_tok", [P, NCH, C])
        w_rout = out_tok[:, 0, 0:KH * NRT].rearrange("p (k e) -> p k e", k=KH)
        w_qkv = sb("w_qkv", [P, KH, 3 * HS])
        b_qkv = sb("b_qkv", [P, 3 * HS])
        qk, v4 = sb("qk", [P, NCH, NQ, QD]), sb("v4", [P, NCH, NQ, QD])
        q_st, k_st = sb("q_st", [P, T], F32R), sb("k_st", [P, T], F32R)
        o_st, w_st = sb("o_st", [P, T], F32R), sb("w_st", [P, C], F32R)
        w_proj = sb("w_proj", [P, C])
        scores = sb("scores", [P, NCH, P])
        causal = sb("causal", [P, P])
        ident = sb("ident", [P, P])
        state = sb("state", [HS, NCH + 1, HS])
        s_st = sb("s_st", [P, NCH, NQ, QD], F32R)
        one_st = sb("one_st", [P, NCH, NQ, QD])
        keep = sb("keep", [HS, 2])
        rt_st = sb("rt_st", [P, KH, P], F32R)
        lg_t = sb("lg_t", [P, T])
        logits = sb("logits", [P, NCH, NRT])
        mhalf = sb("mhalf", [P, NCH])
        shifted = sb("shifted", [P, NCH, NRT])
        expd = sb("expd", [P, NCH, NRT])
        lmax, lsum, linv = sb("lmax", [P, NCH]), sb("lsum", [P, NCH]), sb("linv", [P, NCH])
        probs = sb("probs", [P, NCH, NRT + PAD])
        top8 = sb("top8", [P, NCH, 8])
        chosen = sb("chosen", [P, NCH, 8])
        unchosen = sb("unchosen", [P, NCH, NRT + PAD])
        gate_tok = sb("gate_tok", [P, NCH, NRT])
        bearer = sb("bearer", [P, 1])
        gate_t = sb("gate_t", [NRT, T])
        gate_dram = nc.dram_tensor("gate_dram", [NRT, T], F32).ap()

        acc = [bank(f"acc{i}") for i in range(2)]
        up_ps = [bank(f"up_ps{i}") for i in range(NUP)]
        m0, m1, m2 = (bank(f"m{i}") for i in range(3))

        x_in, small_in, heads_in = sem("x_in"), sem("small_in"), sem("heads_in")
        xt_in = [sem(f"xt_in{i}") for i in range(2)]
        w_in = [sem(f"w_in{c}") for c in range(NWC)]
        gate_out = sem("gate_out")
        gate_in = [sem(f"gate_in{g}") for g in range(NG)]
        out_dma = sem("out_dma")
        CONSTS, FIRST_CONSTS = 16, 5
        consts, w_hi_done, w_lo_done = sem("consts"), sem("w_hi_done"), sem("w_lo_done")
        w_split = [sem(f"w_split{c}") for c in range(NWC)]
        heads_clear, wsum_done = sem("heads_clear"), sem("wsum_done")
        up_done = sem("up_done")
        down_done = sem("down_done")
        acc0_done = sem("acc0_done")
        qkv_ps, qkt_ps, ds_ps, scores_ps = sem("qkv_ps"), sem("qkt_ps"), sem("ds_ps"), sem("scores_ps")
        ot_ps, proj_ps, x1t_ps = sem("ot_ps"), sem("proj_ps"), sem("x1t_ps")
        lgt_ps, logits_ps = sem("lgt_ps"), sem("logits_ps")
        gatet_ps = sem("gatet_ps")
        gelu_done = sem("gelu_done")
        exp_done = sem("exp_done")
        hi_done = sem("hi_done")
        qhi_done, khi_done, ohi_done = sem("qhi_done"), sem("khi_done"), sem("ohi_done")
        shi_done = sem("shi_done")
        gatet_done, lgt_done = sem("gatet_done"), sem("lgt_done")
        x1hi_done = sem("x1hi_done")
        gated = sem("gated")
        lo_done = sem("lo_done")
        qkv_done = sem("qkv_done")
        qk_split, s_split, o_split = sem("qk_split"), sem("s_split"), sem("o_split")
        masked = sem("masked")
        kept = sem("kept")
        state_done = sem("state_done")
        x1lo_done = sem("x1lo_done")
        logits_done, lmax_done, shift_done = sem("logits_done"), sem("lmax_done"), sem("shift_done")
        lsum_done, linv_done = sem("lsum_done"), sem("linv_done")
        probs_done, chosen_done, gate_done = sem("probs_done"), sem("chosen_done"), sem("gate_done")
        top_done, repl_done = sem("top_done"), sem("repl_done")

        class Norm:

            def __init__(self, n):
                self.stats = sb(f"{n}_stats", [P, NCH, 6])
                self.sums = sb(f"{n}_sums", [P, NCH, 2])
                self.apart = sb(f"{n}_apart", [P, NCH])
                self.within = sb(f"{n}_within", [P, NCH])
                self.between = sb(f"{n}_between", [P, NCH])
                self.var = sb(f"{n}_var", [P, NCH])
                self.rstd = sb(f"{n}_rstd", [P, NCH])
                self.shift = sb(f"{n}_shift", [P, NCH])
                self.summed = sem(f"{n}_summed")
                self.stat_done = sem(f"{n}_stat_done")
                self.sums_done = sem(f"{n}_sums_done")
                self.apart_done = sem(f"{n}_apart_done")
                self.within_done = sem(f"{n}_within_done")
                self.between_done = sem(f"{n}_between_done")
                self.var_done = sem(f"{n}_var_done")
                self.rstd_done = sem(f"{n}_rstd_done")
                self.shift_done = sem(f"{n}_shift_done")
                self.done = sem(f"{n}_done")

        ln1, ln2 = Norm("ln1"), Norm("ln2")

        x_v = x.rearrange("(n c p) f -> n p c f", p=P, c=NCH)
        out_v = out.rearrange("(n c p) f -> n p c f", p=P, c=NCH)
        tokens = [slice(c * P, (c + 1) * P) for c in range(NCH)]
        halves = tokens

        def wait(eng, s, count):
            if not isinstance(count, int) or count > 0:
                eng.wait_ge(s, count)

        def staged(c, k):
            at = c % NSTAGE * CHUNK + k * CHUNK // 2
            return stage[:, at:at + CHUNK // 2]

        def chunk(c, up, down):
            es = slice(c * WCH, (c + 1) * WCH)
            return up[:, es].rearrange("p r k e -> p (r k e)"), down[:, es].rearrange("p r f -> p (r f)")

        def sum_heads(eng, level):
            n = HEADS >> level + 1
            if level > 0:
                eng.wait_ge(wsum_done, level)
            dst = w_heads[:, 0:n] if n > 1 else w_proj[:, :].unsqueeze(1)
            eng.tensor_tensor(dst, w_heads[:, 0:n], w_heads[:, n:2 * n], ALU.add).then_inc(wsum_done, 1)

        def split_low(eng, c):
            for k, (hi, lo) in enumerate(zip(chunk(c, up_hi, dn_hi), chunk(c, up_lo, dn_lo))):
                eng.wait_ge(w_hi_done, 2 + 2 * c + k + 1)
                eng.tensor_tensor(lo, staged(c, k), hi.bitcast(F32), ALU.subtract).then_inc(w_split[c], 1)

        def two_halves(ps):
            return ps[:, :].rearrange("p (c f) -> p c f", c=2)

        usual, spare = (m0, m1), (up_ps[2], acc[0])

        block = ctx.enter_context(nc.Block())

        @block.sync
        def _(sp):
            sp.dma_start(x_t[:, 0, :, :], xt[0]).then_inc(xt_in[0], 16)
            sp.dma_start(w_qkv[:, :, :], qkv_wt).then_inc(small_in, 16)
            sp.dma_start(b_qkv[:, :], qkv_b.partition_broadcast(P)).then_inc(small_in, 16)
            sp.dma_start(x_t[:, 1, :, :], xt[1]).then_inc(xt_in[1], 16)
            sp.wait_ge(heads_clear, 1)
            for k in range(NQ):
                sp.dma_start(w_heads[k * QD:k * QD + HS], proj_wt).then_inc(heads_in, 16)
                sp.dma_start(w_heads[k * QD + HS:k * QD + HS + 1, 0, :], proj_b.rearrange("(a f) -> a f", a=1))\
                    .then_inc(heads_in, 16)
            sp.dma_start(w_rout, router_t).then_inc(out_dma, 16)
            sp.dma_start(x_tok[:, :, :], x_v[0]).then_inc(x_in, 16)

            def load_weights(c):
                for k, (src, axes) in enumerate(((up_t, "p r k e -> p (r k e)"), (down_t, "p r f -> p (r f)"))):
                    sp.dma_start(staged(c, k), src[:, c * WCH:(c + 1) * WCH].rearrange(axes)).then_inc(w_in[c], 16)

            def load_xt(p, par):
                wait(sp, qkv_ps, p - 1)
                sp.dma_start(x_t[:, par, :, :], xt[p]).then_inc(xt_in[par], 16)

            def load_x(p):
                wait(sp, ln1.summed, 2 * p)
                sp.dma_start(x_tok[:, :, :], x_v[p]).then_inc(x_in, 16)

            def store(q):
                wait(sp, ln2.done, NCH * (q + 1))
                sp.dma_start(out_v[q], out_tok[:, :, :]).then_inc(out_dma, 16)

            def spread_gates(p):
                for g in range(NG):
                    wait(sp, gate_in[g], 16 * p)
                wait(sp, gatet_done, p + 1)
                sp.dma_start(gate_dram[:, :], gate_t[:, :]).then_inc(gate_out, 16)
                sp.wait_ge(gate_out, 16 * (p + 1))
                for g in range(NG):
                    if g == NG - 1:
                        wait(sp, gated, NRT * p)
                    src = gate_dram[g * GRP:(g + 1) * GRP, :].rearrange("r t -> (r t)").partition_broadcast(P)
                    sp.dma_start(gates[:, g * GRP:(g + 1) * GRP, :].rearrange("p r t -> p (r t)"), src)\
                        .then_inc(gate_in[g], 16)

            for c in range(2):
                load_weights(c)
            sp.wait_ge(wsum_done, LEVELS)
            for c in range(2, NSTAGE):
                load_weights(c)
            load_x(1)
            sp.wait_ge(w_split[0], 2)
            load_weights(NSTAGE)
            load_xt(2, 0)
            for c in range(NWC):
                sp.wait_ge(w_split[c], 2)
            spread_gates(0)
            load_x(2)
            spread_gates(1)

            def tile(t, par):
                load_xt(t + 1, 1 - par)
                store(t - 2)
                load_x(t + 1)
                spread_gates(t)

            with sp.Fori(2, NT - 2, 2) as i:
                tile(i, 0)
                tile(i + 1, 1)
            tile(NT - 2, 0)
            store(NT - 3)
            spread_gates(NT - 1)
            store(NT - 2)
            for i in range(2):
                part = slice(2 * i, 2 * i + 2)
                sp.wait_ge(ln2.done, NCH * (NT - 1) + 2 * (i + 1))
                sp.dma_start(out_v[NT - 1][:, part, :], out_tok[:, part, :]).then_inc(out_dma, 16)
            sp.wait_ge(out_dma, 16 * (NT + 2))

        @block.gpsimd
        def _(pool):
            def zero(buf):
                return pool.memset(buf.bitcast(mybir.dt.uint32), 0)

            for buf in (qk[:, :, :, :], v4[:, :, :, :], ident[:, :]):
                zero(buf).then_inc(consts, 1)
            pool.wait_ge(consts, 3)
            pool.memset(qk[:, :, 0:2, HS:HS + 1], 1.0).then_inc(consts, 1)
            pool.affine_select(out=ident[:, :], in_=ident[:, :], compare_op=ALU.not_equal, fill=1.0,
                               base=0, pattern=[[-1, P]], channel_multiplier=1).then_inc(consts, 1)
            for buf in (keep[:, :], state[:, :, :], rt_st[:, :, :], one_st[:, :, :, :]):
                zero(buf).then_inc(consts, 1)
            for buf, value in ((causal[:, :], 1.0), (mhalf[:, :], -0.5),
                               (probs[:, :, :], -1.0), (chosen[:, :, :], -1.0)):
                pool.memset(buf, value).then_inc(consts, 1)
            pool.wait_ge(consts, 13)
            pool.affine_select(out=causal[:, :], in_=causal[:, :], compare_op=ALU.is_ge, fill=0.0,
                               base=0, pattern=[[1, P]], channel_multiplier=-1).then_inc(consts, 1)
            ones_at = one_st[:, :, :, :].rearrange("p c k j -> p (c k) j")
            pool.affine_select(out=ones_at, in_=ones_at, compare_op=ALU.not_equal, fill=1.0,
                               base=-HS * (2 * QD + 1), pattern=[[0, NCH * NQ], [1, QD]],
                               channel_multiplier=2 * QD).then_inc(consts, 1)
            pool.wait_ge(consts, CONSTS - 1)
            pool.tensor_copy(s_st[:, :, :, :], one_st[:, :, :, :]).then_inc(consts, 1)

            pool.wait_ge(heads_in, 2 * 16 * NQ)
            for level in range(LEVELS - 2):
                sum_heads(pool, level)

            def rstd(ln, n):
                wait(pool, ln.var_done, n + 1)
                pool.tensor_tensor(ln.rstd[:, :], ln.var[:, :], mhalf[:, :], ALU.pow).then_inc(ln.rstd_done, 1)

            split_low(pool, 0)
            rstd(ln1, 0)
            for c in (1, 2, 3, 5):
                split_low(pool, c)
            rstd(ln1, 1)
            with pool.Fori(2, NT) as i:
                rstd(ln2, i - 2)
                rstd(ln1, i)
            rstd(ln2, NT - 2)
            rstd(ln2, NT - 1)

        @block.scalar
        def _(act):
            def front_qk(p, banks=usual):
                wait(act, qkt_ps, p + 1)
                act.activation(q_st[0:2 * QD, :], banks[1][0:2 * QD, :], ACT.Copy).then_inc(qhi_done, 1)
                for k in (0, 2):
                    act.activation(k_st[k * QD:(k + 1) * QD, :], banks[1][2 * QD:3 * QD, :], ACT.Copy).then_inc(khi_done, 1)

            def front_state(p):
                wait(act, state_done, (NCH + 1) * (p + 1))
                for k in (0, 2):
                    act.activation(s_st[k * QD:k * QD + HS, :, :, 0:HS],
                                   state[:, 0:NCH, :].unsqueeze(2).to_broadcast([HS, NCH, NQ, HS]), ACT.Copy)\
                        .then_inc(shi_done, 1)

            def front_o(p, banks=usual):
                wait(act, ot_ps, p + 1)
                act.activation(o_st[:, :], banks[1][:, :], ACT.Copy).then_inc(ohi_done, 1)

            def front_lgt(p):
                wait(act, lgt_ps, p + 1)
                act.activation(lg_t[:, :], m1[:, :], ACT.Copy).then_inc(lgt_done, 1)

            def front_exp(p):
                wait(act, shift_done, p + 1)
                act.activation(expd[:, :, :], shifted[:, :, :], ACT.Exp).then_inc(exp_done, 1)

            def front_x1(p, par):
                wait(act, x1t_ps, p + 1)
                for h, ps in enumerate((m0, m2)):
                    act.activation(x1t_hi[:, par, h, :], ps[:, :], ACT.Copy).then_inc(x1hi_done, 1)

            def front_gate(p):
                wait(act, gatet_ps, p + 1)
                wait(act, gate_out, 16 * p)
                act.activation(gate_t[:, :], m1[0:NRT, :], ACT.Copy).then_inc(gatet_done, 1)

            def high(t, u):
                g = NE * t + u
                if u < NSH:
                    wait(act, gelu_done, g + 1)
                else:
                    wait(act, gated, NRT * t + u - NSH + 1)
                wait(act, down_done, g + 1 - RING)
                act.activation(h_hi[:, u % RING, :], h_gelu[:, u % NUP, :], ACT.Copy).then_inc(hi_done, 1)

            def gelu(t, u):
                wait(act, up_done, NE * t + u + 1)
                wait(act, lo_done, NE * t + u + 1 - NUP)
                act.activation(h_gelu[:, u % NUP, :], up_ps[u % NUP][:, :], ACT.Gelu).then_inc(gelu_done, 1)

            def tile(t, par, first=False, last=False):
                for u in range(OPEN if first else 0, NE):
                    if u > 0:
                        high(t, u - 1)
                    else:
                        high(t - 1, NE - 1)
                    gelu(t, u)
                    if u == 1 and not last:
                        front_qk(t + 1)
                    if u == 2 and not last:
                        front_state(t + 1)
                    if not last:
                        if u == 5:
                            front_o(t + 1)
                        if u == 9 and not first:
                            front_x1(t + 1, 1 - par)
                        if u == 11:
                            front_lgt(t + 1)
                        if u == 12:
                            front_exp(t + 1)
                        if u == 15:
                            front_gate(t + 1)

            front_qk(0)
            act.wait_ge(out_dma, 16)
            act.wait_ge(consts, CONSTS)
            act.activation(rt_st[:, :, 0:NRT], w_rout, ACT.Copy).then_inc(w_hi_done, 1)
            front_state(0)

            def split(c):
                act.wait_ge(w_in[c], 32)
                for k, hi in enumerate(chunk(c, up_hi, dn_hi)):
                    act.activation(hi, staged(c, k), ACT.Copy).then_inc(w_hi_done, 1)

            act.wait_ge(wsum_done, LEVELS)
            act.activation(w_st[:, :], w_proj[:, :], ACT.Copy).then_inc(w_hi_done, 1)
            front_o(0)
            split(0)
            split(1)
            front_qk(1, spare)
            for c in range(2, NWC - 1):
                split(c)
            front_x1(0, 0)
            front_state(1)
            front_lgt(0)
            split(NWC - 1)
            front_exp(0)
            front_o(1, spare)
            front_gate(0)
            gelu(0, 0)
            gelu(0, 1)
            high(0, 0)
            high(0, 1)
            gelu(0, 2)
            gelu(0, 3)
            gelu(0, 4)
            high(0, 2)
            high(0, 3)
            gelu(0, 5)
            high(0, 4)
            front_x1(1, 1)
            tile(0, 0, first=True)
            with act.Fori(1, NT - 1, 2) as i:
                tile(i, 1)
                tile(i + 1, 0)
            tile(NT - 1, 1, last=True)
            high(NT - 1, NE - 1)

        @block.tensor
        def _(pe):
            def front_qkv(p, par, banks=usual):
                wait(pe, xt_in[par], 8 * p + 16 - 8 * par)
                for c in range(NCH):
                    for h in range(KH):
                        mm = pe.matmul(banks[0][:, c * 3 * HS:(c + 1) * 3 * HS], x_t[:, par, h, tokens[c]], w_qkv[:, h, :],
                                       start=h == 0, stop=h == KH - 1)
                mm.then_inc(qkv_ps, 1)

            def front_qkt(p, banks=usual):
                wait(pe, qkv_done, 3 * p + 2)
                if banks is usual:
                    wait(pe, gatet_done, p)
                for c in range(NCH):
                    mm = pe.transpose(banks[1][:, tokens[c]], qk[:, c].rearrange("p k j -> p (k j)"), ident[:, :])
                mm.then_inc(qkt_ps, 1)

            def front_ds(p, banks=usual):
                wait(pe, qkv_done, 3 * (p + 1))
                for c in range(NCH):
                    mm = pe.matmul(banks[0][0:HS, c * HS:(c + 1) * HS], qk[:, c, 2, 0:HS], v4[:, c, 0, 0:HS],
                                   start=True, stop=True)
                mm.then_inc(ds_ps, 1)

            def front_scores(p, banks=usual):
                wait(pe, qk_split, 3 * (p + 1))
                for c in range(NCH):
                    mm = pe.matmul(banks[1][:, tokens[c]], k_st[:, tokens[c]], q_st[:, tokens[c]], start=True, stop=True)
                mm.then_inc(scores_ps, 1)

            def front_out(p, banks=usual):
                wait(pe, masked, p + 1)
                wait(pe, shi_done, 2 * (p + 1))
                wait(pe, s_split, 2 * (p + 1))
                for c in range(NCH):
                    pe.matmul(banks[1][:, tokens[c]], v4[:, c].rearrange("p k j -> p (k j)"), scores[:, c, :],
                              start=True, stop=False)
                    mm = pe.matmul(banks[1][:, tokens[c]], s_st[:, c].rearrange("p k j -> p (k j)"), q_st[:, tokens[c]],
                                   start=False, stop=True)
                mm.then_inc(ot_ps, 1)

            def front_proj(p):
                wait(pe, o_split, p + 1)
                for c in range(NCH):
                    mm = pe.matmul(two_halves((m0, m2)[c // 2])[:, c % 2, :], o_st[:, tokens[c]], w_st[:, :],
                                   start=True, stop=True)
                mm.then_inc(proj_ps, 1)

            def front_x1t(p, par):
                wait(pe, ln1.done, NCH * (p + 1))
                for h in range(KH):
                    for c in range(NCH):
                        mm = pe.transpose((m0, m2)[h][:, tokens[c]], x1_tok[:, par, c, halves[h]], ident[:, :])
                mm.then_inc(x1t_ps, 1)

            def front_lgt(p, par):
                wait(pe, x1lo_done, KH * (p + 1))
                for h in range(KH):
                    for n, b in enumerate((x1t_hi, x1t_lo)):
                        mm = pe.matmul(m1[:, :], rt_st[:, h, :], b[:, par, h, :], start=h + n == 0, stop=h + n == KH)
                mm.then_inc(lgt_ps, 1)

            def front_logits(p):
                wait(pe, lgt_done, p + 1)
                for c in range(NCH):
                    mm = pe.transpose(m1[:, tokens[c]], lg_t[:, tokens[c]], ident[:, :])
                mm.then_inc(logits_ps, 1)

            def front_gatet(p):
                wait(pe, gate_done, p + 1)
                for c in range(NCH):
                    mm = pe.transpose(m1[0:NRT, tokens[c]], gate_tok[:, c, :], ident[:, :])
                mm.then_inc(gatet_ps, 1)

            def up(t, u, par):
                if u == 0:
                    wait(pe, x1lo_done, KH * (t + 1))
                n = 0
                for h in range(KH):
                    for a, b in ((up_hi, x1t_hi), (up_hi, x1t_lo), (up_lo, x1t_hi)):
                        mm = pe.matmul(up_ps[u % NUP][:, :], a[:, u, h, :], b[:, par, h, :],
                                       start=n == 0, stop=n == 3 * KH - 1)
                        n += 1
                mm.then_inc(up_done, 1)

            def down_chunks(u, chunks):
                for c in chunks:
                    for n, (a, b) in enumerate(((h_hi, dn_hi), (h_hi, dn_lo), (h_lo, dn_hi))):
                        mm = pe.matmul(two_halves(acc[c // 2])[:, c % 2, :], a[:, u % RING, tokens[c]], b[:, u, :],
                                       start=u == n == 0 and c % 2 == 0, stop=u == NE - 1 and n == 2 and c % 2 == 1)
                return mm

            def down(t, u):
                wait(pe, lo_done, NE * t + u + 1)
                if u == 0:
                    wait(pe, ln2.summed, 2 * t)
                if u < NE - 1:
                    mm = down_chunks(u, range(NCH))
                else:
                    down_chunks(u, range(NCH // 2)).then_inc(acc0_done, 1)
                    mm = down_chunks(u, range(NCH // 2, NCH))
                mm.then_inc(down_done, 1)

            def first_up(u):
                if u % WCH == 0:
                    pe.wait_ge(w_split[u // WCH], 2)
                if u >= NUP:
                    pe.wait_ge(gelu_done, u + 1 - NUP)
                up(0, u, 0)

            def opening():
                first_up(0)
                front_out(1, spare)
                pe.wait_ge(logits_done, 1)
                front_gatet(0)
                first_up(1)
                front_proj(1)
                pe.wait_ge(state_done, 2 * (NCH + 1))
                first_up(2)
                first_up(3)
                down(0, 0)
                first_up(4)
                down(0, 1)
                first_up(5)
                first_up(6)
                first_up(7)
                front_x1t(1, 1)
                down(0, 2)
                down(0, 3)
                down(0, 4)

            def tile(t, par, first=False, last=False):
                for u in range(OPEN + 2 if first else 0, NE):
                    if first:
                        first_up(u)
                    else:
                        wait(pe, gelu_done, NE * t + u + 1 - NUP)
                        up(t, u, par)
                    p = t + 1
                    if not last:
                        if u == 0:
                            front_qkv(p, 1 - par)
                        if u == 1:
                            front_qkt(p)
                        if u == 2:
                            front_ds(p)
                        if u == 3:
                            front_scores(p)
                    if not last:
                        if u == 5:
                            front_out(p)
                        if u == 6 and not first:
                            front_proj(p)
                        if u == 11:
                            front_lgt(p, 1 - par)
                    if u >= LAG:
                        down(t, u - LAG)
                    elif not first:
                        down(t - 1, NE + u - LAG)
                    if not last:
                        if u == 9 and not first:
                            front_x1t(p, 1 - par)
                        if u == 11:
                            front_logits(p)
                        if u == 15:
                            front_gatet(p)

            pe.wait_ge(small_in, 32)
            front_qkv(0, 0)
            pe.wait_ge(consts, FIRST_CONSTS)
            front_qkt(0)
            front_ds(0)
            front_qkv(1, 1, spare)
            front_scores(0)
            pe.wait_ge(consts, CONSTS)
            front_out(0)
            pe.wait_ge(w_lo_done, 3)
            front_proj(0)
            front_qkt(1, spare)
            front_ds(1, spare)
            front_scores(1, spare)
            front_x1t(0, 0)
            front_lgt(0, 0)
            front_logits(0)
            opening()
            tile(0, 0, first=True)
            with pe.Fori(1, NT - 1, 2) as i:
                tile(i, 1)
                tile(i + 1, 0)
            tile(NT - 1, 1, last=True)
            for i in range(2):
                for u in range(NE - LAG, NE):
                    pe.wait_ge(lo_done, NE * (NT - 1) + u + 1)
                    mm = down_chunks(u, (2 * i, 2 * i + 1))
                mm.then_inc((acc0_done, down_done)[i], (1, LAG)[i])

        @block.vector
        def _(dve):
            def add(ln, i, ps, res):
                dve.tensor_tensor(pre_ln[:, 2 * i:2 * i + 2, :], two_halves(ps), res[:, 2 * i:2 * i + 2, :],
                                  ALU.add).then_inc(ln.summed, 1)

            def stats(ln, n, i):
                wait(dve, ln.summed, 2 * n + i + 1)
                for c in (2 * i, 2 * i + 1):
                    dve.bn_stats(ln.stats[:, c, :], pre_ln[:, c, :]).then_inc(ln.stat_done, 1)

            def moments(ln, n):
                for i in range(2):
                    stats(ln, n, i)
                variance(ln, n)

            def variance(ln, n):
                wait(dve, ln.stat_done, NCH * (n + 1))
                dve.tensor_tensor(ln.sums[:, :, :], ln.stats[:, :, 1:3], ln.stats[:, :, 4:6], ALU.add)\
                    .then_inc(ln.sums_done, 1)
                dve.tensor_tensor(ln.apart[:, :], ln.stats[:, :, 1], ln.stats[:, :, 4], ALU.subtract)\
                    .then_inc(ln.apart_done, 1)
                wait(dve, ln.sums_done, n + 1)
                dve.tensor_scalar(ln.within[:, :], ln.sums[:, :, 1], 1.0 / C, EPS, ALU.mult, ALU.add)\
                    .then_inc(ln.within_done, 1)
                wait(dve, ln.apart_done, n + 1)
                dve.scalar_tensor_tensor(out=ln.between[:, :], in0=ln.apart[:, :], scalar=0.25, in1=ln.apart[:, :],
                                         op0=ALU.mult, op1=ALU.mult).then_inc(ln.between_done, 1)
                wait(dve, ln.within_done, n + 1)
                wait(dve, ln.between_done, n + 1)
                dve.tensor_tensor(ln.var[:, :], ln.within[:, :], ln.between[:, :], ALU.add).then_inc(ln.var_done, 1)

            def normalise(ln, n, dst):
                wait(dve, ln.rstd_done, n + 1)
                dve.scalar_tensor_tensor(out=ln.shift[:, :], in0=ln.sums[:, :, 0], scalar=-0.5, in1=ln.rstd[:, :],
                                         op0=ALU.mult, op1=ALU.mult).then_inc(ln.shift_done, 1)
                wait(dve, ln.shift_done, n + 1)
                for c in range(NCH):
                    dve.tensor_scalar(dst[:, c, :], pre_ln[:, c, :], ln.rstd[:, c:c + 1], ln.shift[:, c:c + 1],
                                      ALU.mult, ALU.add).then_inc(ln.done, 1)

            def front_qkv(p, banks=usual):
                wait(dve, qkv_ps, p + 1)
                ps = banks[0][:, 0:NCH * 3 * HS].rearrange("p (c f) -> p c f", c=NCH)
                for i, (dst, n) in enumerate(((qk[:, :, 0:2, 0:HS], 2), (qk[:, :, 2:4, 0:HS], 2), (v4[:, :, :, 0:HS], NQ))):
                    part = slice(i * HS, (i + 1) * HS)
                    dve.tensor_tensor(dst, ps[:, :, part].unsqueeze(2).to_broadcast([P, NCH, n, HS]),
                                      b_qkv[:, part].unsqueeze(1).unsqueeze(1).to_broadcast([P, NCH, n, HS]),
                                      ALU.add).then_inc(qkv_done, 1)

            def front_qk(p, banks=usual):
                wait(dve, qhi_done, p + 1)
                dve.tensor_tensor(q_st[2 * QD:P, :], banks[1][0:2 * QD, :], q_st[0:2 * QD, :].bitcast(F32), ALU.subtract)\
                    .then_inc(qk_split, 1)
                wait(dve, khi_done, 2 * (p + 1))
                for k in (1, 3):
                    dve.tensor_tensor(k_st[k * QD:(k + 1) * QD, :], banks[1][2 * QD:3 * QD, :],
                                      k_st[2 * QD:3 * QD, :].bitcast(F32), ALU.subtract).then_inc(qk_split, 1)

            def lo_part(st, src, a, b):
                return dve.tensor_tensor(st[a:b, :], src[a:b, :], st[a:b, :].bitcast(F32), ALU.subtract)

            def front_o(p, banks=usual):
                wait(dve, ohi_done, p + 1)
                lo_part(o_st, banks[1], 2 * QD, P).then_inc(o_split, 1)

            def front_state(p, even, banks=usual):
                wait(dve, ds_ps, p + 1)
                wait(dve, state_done, (NCH + 1) * p)
                wait(dve, kept, p)
                wait(dve, ot_ps, p)
                if even:
                    dve.tensor_scalar(state[:, 0, :], state[:, NCH, :], keep[:, 0:1], None, ALU.mult)\
                        .then_inc(state_done, 1)
                else:
                    dve.tensor_copy(state[:, 0, :], state[:, NCH, :]).then_inc(state_done, 1)
                for c in range(NCH):
                    wait(dve, state_done, (NCH + 1) * p + c + 1)
                    dve.tensor_tensor(state[:, c + 1, :], banks[0][0:HS, c * HS:(c + 1) * HS], state[:, c, :], ALU.add)\
                        .then_inc(state_done, 1)
                wait(dve, shi_done, 2 * p + 1)
                for k in (1, 3):
                    dve.tensor_tensor(s_st[k * QD:k * QD + HS, :, :, 0:HS],
                                      state[:, 0:NCH, :].unsqueeze(2).to_broadcast([HS, NCH, NQ, HS]),
                                      s_st[0:HS, :, :, 0:HS].bitcast(F32), ALU.subtract).then_inc(s_split, 1)
                if even:
                    dve.tensor_scalar(keep[:, 1:2], keep[:, 0:1], -1.0, 1.0, ALU.mult, ALU.add).then_inc(kept, 1)
                else:
                    dve.tensor_copy(keep[:, 0:1], keep[:, 1:2]).then_inc(kept, 1)

            def front_mask(p, banks=usual):
                wait(dve, scores_ps, p + 1)
                dve.tensor_tensor(scores[:, :, :], banks[1][:, :].rearrange("p (c t) -> p c t", c=NCH),
                                  causal[:, :].unsqueeze(1).to_broadcast([P, NCH, P]), ALU.mult).then_inc(masked, 1)

            def front_add(p):
                wait(dve, proj_ps, p + 1)
                wait(dve, x_in, 16 * (p + 1))
                wait(dve, ln2.done, NCH * (p - 1))
                for i, ps in enumerate((m0, m2)):
                    add(ln1, i, ps, x_tok)

            def front_x1lo(p, par):
                for h, ps in enumerate((m0, m2)):
                    wait(dve, x1hi_done, KH * p + h + 1)
                    dve.tensor_tensor(x1t_lo[:, par, h, :], ps[:, :], x1t_hi[:, par, h, :].bitcast(F32), ALU.subtract)\
                        .then_inc(x1lo_done, 1)

            def router_shift(p):
                wait(dve, logits_ps, p + 1)
                ps = m1[:, :].rearrange("p (c k j) -> p c j k", c=NCH, k=NQ)
                dve.tensor_reduce(logits[:, :, :], ps[:, :, 0:NRT, 0:2], AX.X, ALU.add).then_inc(logits_done, 1)
                wait(dve, logits_done, p + 1)
                dve.tensor_reduce(lmax[:, :], logits[:, :, :], AX.X, ALU.max).then_inc(lmax_done, 1)
                wait(dve, lmax_done, p + 1)
                dve.tensor_tensor(shifted[:, :, :], logits[:, :, :],
                                  lmax[:, :].unsqueeze(2).to_broadcast([P, NCH, NRT]), ALU.subtract)\
                    .then_inc(shift_done, 1)

            def router_gate(p):
                wait(dve, exp_done, p + 1)
                dve.tensor_reduce(lsum[:, :], expd[:, :, :], AX.X, ALU.add).then_inc(lsum_done, 1)
                wait(dve, lsum_done, p + 1)
                dve.reciprocal(linv[:, :], lsum[:, :]).then_inc(linv_done, 1)
                wait(dve, linv_done, p + 1)
                dve.tensor_tensor(probs[:, :, 0:NRT], expd[:, :, :],
                                  linv[:, :].unsqueeze(2).to_broadcast([P, NCH, NRT]), ALU.mult).then_inc(probs_done, 1)
                wait(dve, probs_done, p + 1)
                dve.memset(bearer[:, :], 0.0)
                for c in range(NCH):
                    dve.max(top8[:, c, :], probs[:, c, 0:NRT]).then_inc(top_done, 1)
                wait(dve, top_done, NCH * (p + 1))
                dve.tensor_copy(chosen[:, :, 0:TOPK], top8[:, :, 0:TOPK]).then_inc(chosen_done, 1)
                wait(dve, chosen_done, p + 1)
                dve.memset(bearer[:, :], 0.0)
                for c in range(NCH):
                    dve.match_replace(unchosen[:, c, :], chosen[:, c, :], probs[:, c, :], 0.0).then_inc(repl_done, 1)
                wait(dve, repl_done, NCH * (p + 1))
                dve.tensor_tensor(gate_tok[:, :, :], probs[:, :, 0:NRT], unchosen[:, :, 0:NRT], ALU.subtract)\
                    .then_inc(gate_done, 1)

            def back_add(q, par, i, last=False):
                if i == 0:
                    wait(dve, ln1.done, NCH * (q + 2) if not last else NCH * NT)
                    wait(dve, acc0_done, q + 1)
                else:
                    wait(dve, down_done, NE * (q + 1))
                add(ln2, i, acc[i], x1_tok[:, par])

            def back_out(q):
                wait(dve, out_dma, 16 * (q + 1))
                normalise(ln2, q, out_tok)

            def low(t, u):
                wait(dve, hi_done, NE * t + u + 1)
                dve.tensor_tensor(h_lo[:, u % RING, :], h_gelu[:, u % NUP, :], h_hi[:, u % RING, :].bitcast(F32),
                                  ALU.subtract).then_inc(lo_done, 1)

            def gate(t, u):
                r = u - NSH
                if r % GRP == 0:
                    wait(dve, gate_in[r // GRP], 16 * (t + 1))
                wait(dve, gelu_done, NE * t + u + 1)
                dve.tensor_tensor(h_gelu[:, u % NUP, :], h_gelu[:, u % NUP, :], gates[:, r, :], ALU.mult)\
                    .then_inc(gated, 1)

            def tile(t, par, first=False, last=False):
                for u in range(OPEN if first else 0, NE):
                    if u > 0:
                        low(t, u - 1)
                    else:
                        low(t - 1, NE - 1)
                    p = t + 1
                    if u == 5 and not last:
                        front_o(p)
                    if u >= NSH:
                        gate(t, u)
                    if not last:
                        if u == 0:
                            front_qkv(p)
                        if u == 1:
                            front_qk(p)
                    if not first:
                        if u == 2:
                            for i in range(2):
                                back_add(t - 1, 1 - par, i)
                    if not last:
                        if u == 2:
                            front_state(p, even=par == 1)
                        if u == 3:
                            front_mask(p)
                    if not first:
                        if u == 4:
                            moments(ln2, t - 1)
                    if u == 5 and not first:
                        back_out(t - 1)
                    if not last:
                        if u == 6 and not first:
                            front_add(p)
                            moments(ln1, p)
                        if u == 7 and not first:
                            normalise(ln1, p, x1_tok[:, 1 - par])
                        if u == 9 and not first:
                            front_x1lo(p, 1 - par)
                        if u == 11:
                            router_shift(p)
                        if u == 13:
                            router_gate(p)

            dve.memset(w_heads, 0.0).then_inc(heads_clear, 1)
            dve.wait_ge(small_in, 32)
            dve.wait_ge(consts, FIRST_CONSTS)
            front_qkv(0)
            front_qk(0)
            dve.wait_ge(consts, CONSTS)
            front_state(0, even=True)
            front_mask(0)
            for level in range(LEVELS - 2, LEVELS):
                sum_heads(dve, level)
            dve.wait_ge(w_hi_done, 1)
            dve.tensor_tensor(rt_st[:, :, QD:QD + NRT], w_rout, rt_st[:, :, 0:NRT].bitcast(F32), ALU.subtract)\
                .then_inc(w_lo_done, 1)
            dve.wait_ge(w_hi_done, 2)
            lo_part(w_st, w_proj, QD, 2 * QD).then_inc(w_lo_done, 1)
            lo_part(w_st, w_proj, 3 * QD, P).then_inc(w_lo_done, 1)
            front_o(0)
            front_qkv(1, spare)
            front_add(0)
            moments(ln1, 0)
            front_qk(1, spare)
            normalise(ln1, 0, x1_tok[:, 0])
            front_mask(1, spare)
            front_x1lo(0, 0)
            front_state(1, False, spare)
            split_low(dve, 4)
            router_shift(0)
            router_gate(0)
            front_o(1, spare)
            front_add(1)
            low(0, 0)
            low(0, 1)
            moments(ln1, 1)
            normalise(ln1, 1, x1_tok[:, 1])
            gate(0, 2)
            gate(0, 3)
            low(0, 2)
            gate(0, 4)
            low(0, 3)
            low(0, 4)
            gate(0, 5)
            front_x1lo(1, 1)
            tile(0, 0, first=True)
            with dve.Fori(1, NT - 1, 2) as i:
                tile(i, 1)
                tile(i + 1, 0)
            tile(NT - 1, 1, last=True)
            low(NT - 1, NE - 1)
            for i in range(2):
                back_add(NT - 1, 1, i, last=True)
                stats(ln2, NT - 1, i)
            variance(ln2, NT - 1)
            back_out(NT - 1)


def kernel(L0_attn_ids, L0_attn_qkv_w, L0_attn_qkv_b, L0_attn_proj_w, L0_attn_proj_b, L0_ffn_shared_up,
           L0_ffn_shared_down, L0_ffn_routed_up, L0_ffn_routed_down, L0_ffn_router_w):
    import numpy as np
    import concourse.bacc as bacc
    from concourse.bass_utils import run_bass_kernel_spmd

    def halved(w):
        return np.asarray(w).reshape(-1, KH, P).transpose(2, 1, 0)

    x = np.asarray(L0_attn_ids).reshape(B * SEQ, C)
    up = np.concatenate([np.asarray(L0_ffn_shared_up), np.asarray(L0_ffn_routed_up)])
    down = np.concatenate([np.asarray(L0_ffn_shared_down), np.asarray(L0_ffn_routed_down)])
    arrays = {
        "x": x,
        "xt": x.reshape(NT, T, KH, P).transpose(0, 3, 2, 1),
        "qkv_wt": halved(L0_attn_qkv_w),
        "qkv_b": np.asarray(L0_attn_qkv_b),
        "proj_wt": np.asarray(L0_attn_proj_w).reshape(C, HEADS, HS).transpose(2, 1, 0),
        "proj_b": np.asarray(L0_attn_proj_b),
        "up_t": up.reshape(NE, P, KH, P).transpose(3, 0, 2, 1),
        "down_t": down.transpose(2, 0, 1),
        "router_t": halved(L0_ffn_router_w),
    }
    arrays = {name: np.ascontiguousarray(a) for name, a in arrays.items()}
    nc = bacc.Bacc("TRN2", target_bir_lowering=False, num_devices=1)
    args = [nc.dram_tensor(name, a.shape, F32, kind="ExternalInput").ap() for name, a in arrays.items()]
    out = nc.dram_tensor("out", (B * SEQ, C), F32, kind="ExternalOutput").ap()
    build(nc, *args, out)
    got = run_bass_kernel_spmd(nc, [arrays], core_ids=[0])
    return got.results[0]["out"].reshape(B, SEQ, C)
```
